# Optimizing a Trainium2 kernel written in Bass

```python
import numpy as np
import jax
import jax.numpy as jnp

def _softmax(x, axis=-1):
    return jax.nn.softmax(x, axis=axis)

def _gelu(x):
    return jax.nn.gelu(x, approximate=True)

def _silu(x):
    return jax.nn.silu(x)

def _sigmoid(x):
    return jax.nn.sigmoid(x)

def _layernorm(x, axis=-1, eps=1e-05):
    m = jnp.mean(x, axis=axis, keepdims=True)
    v = jnp.var(x, axis=axis, keepdims=True)
    return (x - m) / jnp.sqrt(v + eps)

def _scatter_add(tgt, idx, src, axis=0):
    return tgt.at[idx].add(src)

def _segment_sum(src, seg, n):
    return jax.ops.segment_sum(src, seg, n)
kernel_name = 'mk_macaron_d1_jaxref_r8_0254e3'

def setup_inputs(seed: int=0):
    np.random.seed(seed)
    _w = jnp.asarray

    def _L0_attn_setup():
        import jax, jax.numpy as jnp
        import numpy as np
        B, S, H = (4, 256, 256)
        key = jax.random.key(seed)
        k1, k2, k3 = jax.random.split(key, 3)
        xav_qkv = float(np.sqrt(6.0 / (H + 3 * H)))
        xav_out = float(np.sqrt(6.0 / (H + H)))
        return {'hidden_states': jax.random.normal(k1, (B, S, H), dtype=jnp.float32), 'w_qkv': jax.random.uniform(k2, (3 * H, H), minval=-xav_qkv, maxval=xav_qkv, dtype=jnp.float32), 'b_qkv': jnp.zeros((3 * H,), dtype=jnp.float32), 'w_out': jax.random.uniform(k3, (H, H), minval=-xav_out, maxval=xav_out, dtype=jnp.float32), 'b_out': jnp.zeros((H,), dtype=jnp.float32)}
    _L0_attn_in = _L0_attn_setup()

    def _L0_ffn_setup():
        import jax, jax.numpy as jnp
        import numpy as np
        TOP_K = 6
        CAP_FACTOR = 2

        def _shared_swiglu(x, wg, wu, wd):
            return jax.nn.silu(x @ wg.T) * (x @ wu.T) @ wd.T
        key = jax.random.key(seed)
        ks = jax.random.split(key, 8)
        B, S, D, E, F, FS = (4, 256, 256, 64, 176, 352)
        scale = jnp.float32(0.02)
        return {'hidden_states': jax.random.normal(ks[0], (B, S, D), jnp.float32), 'gate_w': jax.random.normal(ks[1], (E, D), jnp.float32) * scale, 'w_gate': jax.random.normal(ks[2], (E, F, D), jnp.float32) * scale, 'w_up': jax.random.normal(ks[3], (E, F, D), jnp.float32) * scale, 'w_down': jax.random.normal(ks[4], (E, D, F), jnp.float32) * scale, 'sh_gate': jax.random.normal(ks[5], (FS, D), jnp.float32) * scale, 'sh_up': jax.random.normal(ks[6], (FS, D), jnp.float32) * scale, 'sh_down': jax.random.normal(ks[7], (D, FS), jnp.float32) * scale}
    _L0_ffn_in = _L0_ffn_setup()
    _d = {'L0_attn_hidden_states': _L0_attn_in['hidden_states'], 'L0_attn_w_qkv': _L0_attn_in['w_qkv'], 'L0_attn_b_qkv': _L0_attn_in['b_qkv'], 'L0_attn_w_out': _L0_attn_in['w_out'], 'L0_attn_b_out': _L0_attn_in['b_out'], 'L0_ffn_gate_w': _L0_ffn_in['gate_w'], 'L0_ffn_w_gate': _L0_ffn_in['w_gate'], 'L0_ffn_w_up': _L0_ffn_in['w_up'], 'L0_ffn_w_down': _L0_ffn_in['w_down'], 'L0_ffn_sh_gate': _L0_ffn_in['sh_gate'], 'L0_ffn_sh_up': _L0_ffn_in['sh_up'], 'L0_ffn_sh_down': _L0_ffn_in['sh_down']}
    _x0 = _d['L0_attn_hidden_states']
    _d['L0_attn_hidden_states'] = jax.random.normal(jax.random.fold_in(jax.random.key(seed), 1), (4, 512, 256), dtype=_x0.dtype)
    del _x0
    return _d

def reference(L0_attn_hidden_states, L0_attn_w_qkv, L0_attn_b_qkv, L0_attn_w_out, L0_attn_b_out, L0_ffn_gate_w, L0_ffn_w_gate, L0_ffn_w_up, L0_ffn_w_down, L0_ffn_sh_gate, L0_ffn_sh_up, L0_ffn_sh_down):

    def _L0_attn_ref(hidden_states, w_qkv, b_qkv, w_out, b_out):
        import jax, jax.numpy as jnp
        import numpy as np
        B, S, H = (4, 256, 256)
        Bc, Sc, Hc = hidden_states.shape
        scaling = jnp.sqrt(jnp.asarray(Hc, hidden_states.dtype))
        qkv = jnp.einsum('bsh,oh->bso', hidden_states, w_qkv) + b_qkv
        q, k, v = jnp.split(qkv, 3, axis=-1)
        scores = jnp.einsum('bqh,bkh->bqk', q, k) / scaling
        probs = jax.nn.softmax(scores, axis=-1)
        context = jnp.einsum('bqk,bkh->bqh', probs, v)
        out = jnp.einsum('bsh,oh->bso', context, w_out) + b_out
        return out

    def _L0_ffn_ref(hidden_states, gate_w, w_gate, w_up, w_down, sh_gate, sh_up, sh_down):
        import jax, jax.numpy as jnp
        import numpy as np
        TOP_K = 6
        CAP_FACTOR = 2

        def _shared_swiglu(x, wg, wu, wd):
            return jax.nn.silu(x @ wg.T) * (x @ wu.T) @ wd.T
        B, S, D = hidden_states.shape
        E = gate_w.shape[0]
        x = hidden_states.reshape(-1, D)
        N = x.shape[0]
        A = N * TOP_K
        C = CAP_FACTOR * ((A + E - 1) // E)
        scores = jax.nn.softmax(x @ gate_w.T, axis=-1)
        topk_w, topk_idx = jax.lax.top_k(scores, TOP_K)
        topk_w = topk_w / (topk_w.sum(-1, keepdims=True) + 1e-20)
        flat_e = topk_idx.reshape(-1)
        flat_w = topk_w.reshape(-1)
        order = jnp.argsort(flat_e)
        se = flat_e[order]
        st = order // TOP_K
        sw = flat_w[order]
        counts = jnp.bincount(flat_e, length=E)
        offsets = jnp.cumsum(counts) - counts
        pos = jnp.arange(A) - offsets[se]
        valid = pos < C
        pos_c = jnp.minimum(pos, C - 1)
        buf = jnp.zeros((E, C, D), x.dtype).at[se, pos_c].add(jnp.where(valid[:, None], x[st], jnp.zeros((), x.dtype)))
        g = jnp.einsum('ecd,efd->ecf', buf, w_gate)
        u = jnp.einsum('ecd,efd->ecf', buf, w_up)
        eo = jnp.einsum('ecf,edf->ecd', jax.nn.silu(g) * u, w_down)
        gathered = eo[se, pos_c] * (sw * valid.astype(sw.dtype))[:, None]
        y = jnp.zeros_like(x).at[st].add(gathered).reshape(B, S, D)
        return y + _shared_swiglu(hidden_states, sh_gate, sh_up, sh_down)
    x = L0_attn_hidden_states
    x = x + 0.5 * _L0_ffn_ref(_layernorm(x, axis=-1), L0_ffn_gate_w, L0_ffn_w_gate, L0_ffn_w_up, L0_ffn_w_down, L0_ffn_sh_gate, L0_ffn_sh_up, L0_ffn_sh_down)
    x = x + _L0_attn_ref(_layernorm(x, axis=-1), L0_attn_w_qkv, L0_attn_b_qkv, L0_attn_w_out, L0_attn_b_out)
    x = x + 0.5 * _L0_ffn_ref(_layernorm(x, axis=-1), L0_ffn_gate_w, L0_ffn_w_gate, L0_ffn_w_up, L0_ffn_w_down, L0_ffn_sh_gate, L0_ffn_sh_up, L0_ffn_sh_down)
    return x

_drawn_inputs = setup_inputs


def setup_inputs(seed=0):
    import zlib

    import numpy as np

    out = dict(_drawn_inputs(seed))
    spreads = {'L0_attn_b_qkv': (0.0, 0.1), 'L0_attn_b_out': (0.0, 0.1)}
    factors = {'L0_ffn_gate_w': 8.0,
     'L0_ffn_w_gate': 8.0,
     'L0_ffn_w_up': 8.0,
     'L0_ffn_w_down': 8.0,
     'L0_ffn_sh_gate': 2.972,
     'L0_ffn_sh_up': 2.946,
     'L0_ffn_sh_down': 2.945}
    for name, (base, spread) in spreads.items():
        noise = np.random.default_rng([zlib.crc32(name.encode()), seed]).standard_normal(out[name].shape)
        drawn = base * np.exp(spread * noise) if base else spread * noise
        out[name] = jnp.asarray(drawn.astype(out[name].dtype))
    for name, factor in factors.items():
        out[name] = (out[name] * factor).astype(out[name].dtype)
    return out
```

```python
from contextlib import ExitStack

import numpy as np

import concourse.bass as bass
from concourse import mybir

F32 = mybir.dt.float32
BF16 = mybir.dt.bfloat16
I32 = mybir.dt.int32
U32 = mybir.dt.uint32
ALU = mybir.AluOpType
ACT = mybir.ActivationFunctionType
AX = mybir.AxisListType

P = 128
B, S, D = 4, 512, 256
N = B * S
E, F, FS, TOP_K, CAP_FACTOR = 64, 176, 352, 6, 2
CAP = CAP_FACTOR * ((N * TOP_K + E - 1) // E)
EPS = 1e-5

KD = D // P
TILES = N // P
GROUPS = B
GT = TILES // GROUPS
FH = F // 2
CT = CAP // P
SLOTS = E * CAP
STEPS = E * CT
ROW = D + 4
SENT = N * TOP_K
NOWHERE = 1 << 20
FC = [(0, 128), (128, 128), (256, FS - 256)]
FFNS = 2
W_BUFS = 4
UNROLL = W_BUFS * CT
ROUNDS = E // W_BUFS
BLANK_ROWS = SLOTS // ROUNDS // P
Y_BUFS = 4
assert CAP % P == 0 and STEPS % UNROLL == 0 and GT == 4 and KD == 2


class Tally:

    def __init__(self, sem):
        self.sem, self.base, self.n = sem, 0, 0

    def add(self, instruction):
        self.n += 1
        instruction.then_inc(self.sem, 1)
        return self.n

    def at(self, n):
        return self.base + n


def build(nc, x, wqkv, woT, bqk, bv, bo, gateT, w_gu, w_d, sh_g, sh_u, sh_d, out):
    slot_rows = [nc.dram_tensor(f"slot_rows{f}", (SLOTS, ROW), F32).ap() for f in range(FFNS)]
    results = nc.dram_tensor("results", (SENT, D), F32).ap()

    with ExitStack() as ctx:
        def sb(name, shape, dt=F32):
            return ctx.enter_context(nc.sbuf_tensor(name, shape, dt))

        def sem(name):
            return ctx.enter_context(nc.semaphore(name))

        x_res = sb("x_res", [P, TILES, D])
        wqkv_sb = sb("wqkv_sb", [P, KD, 3 * D])
        wo_sb = sb("wo_sb", [P, KD, D])
        bqk_sb = sb("bqk_sb", [P, 4])
        bv_sb = sb("bv_sb", [P, D])
        bo_sb = sb("bo_sb", [P, D])
        gate_sb = sb("gate_sb", [P, KD, E])
        shg_sb = sb("shg_sb", [P, KD, FS])
        shu_sb = sb("shu_sb", [P, KD, FS])
        shd_sb = sb("shd_sb", [P, len(FC), D])
        ident = sb("ident", [P, P])
        earlier = sb("earlier", [P, P], BF16)
        ones = sb("ones", [P, P], BF16)
        slot_base = sb("slot_base", [P, E])
        result_row = sb("result_row", [P, TILES, TOP_K], I32)
        blank = sb("blank", [P, BLANK_ROWS, ROW])
        eps = sb("eps", [P, 1])
        stats = sb("stats", [P, GT, 6])
        mv = sb("mv", [P, GT, 2])
        std = sb("std", [P, GT])
        rstd = sb("rstd", [P, GT])
        row = sb("row", [P, GT, TOP_K, ROW])
        xnT = sb("xnT", [P, KD, S])
        top_logits = sb("top_logits", [P, GT, 8])
        neg_max = sb("neg_max", [P, GT])
        expl = sb("expl", [P, GT, E])
        expsum = sb("expsum", [P, GT])
        rexpsum = sb("rexpsum", [P, GT])
        probs = sb("probs", [P, GT, E + 2])
        top = sb("top", [P, GT, 8])
        chosen = sb("chosen", [P, GT, 8])
        topsum = sb("topsum", [P, GT])
        rtop = sb("rtop", [P, GT])
        marked = sb("marked", [P, GT, E + 2])
        mask = sb("mask", [P, GT, E], BF16)
        before = sb("before", [P, GT, E], BF16)
        kept = sb("kept", [P, GT, E])
        key = sb("key", [P, GT, E])
        wkept = sb("wkept", [P, GT, E])
        top_keys = sb("top_keys", [P, GT, 8])
        is_key = sb("is_key", [P, GT, TOP_K, E])
        w_row = sb("w_row", [P, GT, TOP_K])
        w_tok = sb("w_tok", [P, TILES, TOP_K])
        absent = sb("absent", [P, GT, TOP_K])
        slot_f = sb("slot_f", [P, GT, TOP_K])
        slot_idx = sb("slot_idx", [P, GT, TOP_K], U32)
        sh_act = sb("sh_act", [P, S])
        sh_h = sb("sh_h", [P, len(FC), S])
        wgu_sb = sb("wgu_sb", [P, W_BUFS, KD, 2 * F])
        wd_sb = sb("wd_sb", [FH, W_BUFS, 2, D])
        slots_sb = sb("slots_sb", [P, W_BUFS, CT, ROW])
        xT = sb("xT", [P, 2, KD, P])
        act_g = sb("act_g", [P, 2, F])
        h = sb("h", [P, 2, F])
        hT = sb("hT", [FH, 2, 2, P])
        y_sb = sb("y_sb", [P, Y_BUFS, D])
        back = sb("back", [P, 2, TOP_K, D])
        xa = sb("xa", [P, GT, D])
        xaT = sb("xaT", [P, KD, S])
        qkT = sb("qkT", [P, 4, S])
        v_sb = sb("v_sb", [P, GT, D])
        row_max = sb("row_max", [P, GT])
        neg_row_max = sb("neg_row_max", [P, GT])
        attn = sb("attn", [P, GT, S])
        attn_sum = sb("attn_sum", [P, GT])
        rattn = sb("rattn", [P, GT])
        attnT = sb("attnT", [P, GT, S])
        ctxT = sb("ctxT", [P, KD, S])

        bank = [ctx.enter_context(nc.psum_tensor(f"bank{i}", [P, 512], F32)) for i in range(8)]

        s_load = sem("s_load")
        s_x = sem("s_x")
        s_const = sem("s_const")
        s_blank = sem("s_blank")
        s_blank_set = sem("s_blank_set")
        s_pool = sem("s_pool")
        s_sent = [sem(f"s_sent{j}") for j in range(GT)]
        s_dve = sem("s_dve")
        s_var = sem("s_var")
        s_std = sem("s_std")
        s_row = sem("s_row")
        s_rowT = sem("s_rowT")
        s_xnT = sem("s_xnT")
        s_logits = sem("s_logits")
        s_negmax = sem("s_negmax")
        s_expl = sem("s_expl")
        s_mask = sem("s_mask")
        s_before = sem("s_before")
        s_pos = sem("s_pos")
        s_slot = sem("s_slot")
        s_shgu = sem("s_shgu")
        s_shact = sem("s_shact")
        s_shh = sem("s_shh")
        s_shout = sem("s_shout")
        s_shadd = sem("s_shadd")
        s_slots = [sem(f"s_slots{i}") for i in range(W_BUFS)]
        s_wgu = [sem(f"s_wgu{i}") for i in range(W_BUFS)]
        s_wd = [sem(f"s_wd{i}") for i in range(W_BUFS)]
        s_xT_ps = sem("s_xT_ps")
        s_xT = sem("s_xT")
        s_gu = sem("s_gu")
        s_act = sem("s_act")
        s_h = sem("s_h")
        s_hT_ps = sem("s_hT_ps")
        s_hT = sem("s_hT")
        s_y_ps = sem("s_y_ps")
        s_y = sem("s_y")
        s_result = [sem(f"s_result{i}") for i in range(Y_BUFS)]
        s_back = [sem(f"s_back{i}") for i in range(2)]
        s_added = sem("s_added")
        s_avar = sem("s_avar")
        s_astd = sem("s_astd")
        s_xa = sem("s_xa")
        s_xaT_ps = sem("s_xaT_ps")
        s_xaT = sem("s_xaT")
        s_qk_ps = sem("s_qk_ps")
        s_qk = sem("s_qk")
        s_v_ps = sem("s_v_ps")
        s_v = sem("s_v")
        s_score = sem("s_score")
        s_rowmax = sem("s_rowmax")
        s_attn = sem("s_attn")
        s_attnT_ps = sem("s_attnT_ps")
        s_attnT = sem("s_attnT")
        s_ctx_ps = sem("s_ctx_ps")
        s_ctx = sem("s_ctx")
        s_o_ps = sem("s_o_ps")
        s_out = sem("s_out")
        block = ctx.enter_context(nc.Block())

        rowT_ps = bank[0:2]
        logits_ps = bank[2]
        pos_ps = bank[3]
        shg_ps, shu_ps = bank[4], bank[5]
        sho_ps = bank[6:8]
        xT_ps, gu_ps, hT_ps, y_ps = bank[0:2], bank[2:4], bank[4:6], bank[6:8]

        def wait_alone(eng, sem_, value):
            eng.wait_ge(sem_, value)
            eng.nop(nofuse=True)

        def pipeline(eng, f, stages):
            lead = len(stages) - 1

            def turn(s, at_of):
                for i, stage in enumerate(stages):
                    at = at_of(s - i)
                    if stage is not None and at is not None:
                        t = (s - i) % UNROLL
                        stage(t, at, t // CT, t % CT)

            def peeled(t):
                if not 0 <= t < STEPS:
                    return None
                r = t // UNROLL
                return {"base": f * STEPS + r * UNROLL, "round": f * ROUNDS + r + 1,
                        "full": f > 0 or t >= 2, "y_full": f > 0 or t >= Y_BUFS}

            for s in range(UNROLL):
                turn(s, peeled)
            with eng.Fori(1, ROUNDS) as r:
                for s in range(UNROLL):
                    def looped(t):
                        back_one = t < 0
                        return {"base": r * UNROLL + (f * STEPS - (UNROLL if back_one else 0)),
                                "round": r + (f * ROUNDS + (0 if back_one else 1)),
                                "full": True, "y_full": True}
                    turn(s, looped)
            for s in range(STEPS, STEPS + lead):
                turn(s, peeled)

        LOADS = 11

        @block.sync
        def _(sp):
            for g in range(GROUPS):
                sp.dma_start(x_res[:, g * GT:(g + 1) * GT, :],
                             x[g * S:(g + 1) * S, :].rearrange("(t p) d -> p t d", p=P)).then_inc(s_x, 16)
            for dst, src in ((gate_sb, gateT), (shg_sb, sh_g), (shu_sb, sh_u), (wqkv_sb, wqkv), (wo_sb, woT)):
                sp.dma_start(dst[:, :, :], src).then_inc(s_load, 16)
            for c, (f0, fn) in enumerate(FC):
                sp.dma_start(shd_sb[0:fn, c, :], sh_d[f0:f0 + fn, :]).then_inc(s_load, 16)
            for dst, src in ((bqk_sb, bqk), (bv_sb, bv), (bo_sb, bo)):
                sp.dma_start(dst[:, :], src).then_inc(s_load, 16)
            sp.wait_ge(s_blank_set, 2)
            first = slot_rows[0].rearrange("(r p n) c -> r p n c", p=P, n=BLANK_ROWS)
            for r in range(ROUNDS):
                sp.dma_start(first[r], blank[:, :, :]).then_inc(s_blank, 16)
            res = results.rearrange("(r p n) c -> r p n c", p=P, n=BLANK_ROWS)
            for r in range(SENT // P // BLANK_ROWS):
                sp.dma_start(res[r], blank[:, :, 0:D]).then_inc(s_blank, 16)
            second = slot_rows[1].rearrange("(r p n) c -> (r p) n c", p=P, n=BLANK_ROWS)

            for f in range(FFNS):
                rows = slot_rows[f].rearrange("(c p) r -> p c r", p=P)
                for j in range(GT):
                    sp.wait_ge(s_sent[j], 16 * TOP_K * GROUPS * (f + 1))

                def load_expert(b, e, freed):
                    if freed is not None:
                        wait_alone(sp, s_gu, freed + CT)
                    sp.dma_start(wgu_sb[:, b, :, :], w_gu[bass.ds(e * P, P), :, :]).then_inc(s_wgu[b], 16)
                    if freed is not None:
                        wait_alone(sp, s_y_ps, freed + CT)
                    sp.dma_start(wd_sb[:, b, :, :], w_d[bass.ds(e * FH, FH), :, :]).then_inc(s_wd[b], 16)
                    if freed is not None:
                        for k in range(CT):
                            t = (b * CT + k)
                            wait_alone(sp, s_result[t % Y_BUFS], freed_results[0] + 16 * (t // Y_BUFS + 1))
                    sp.dma_start(slots_sb[:, b, :, :], rows[:, bass.ds(e * CT, CT), :]).then_inc(s_slots[b], 16)

                freed_results = [0]
                for b in range(W_BUFS):
                    freed_results[0] = 16 * (UNROLL // Y_BUFS) * (ROUNDS * f - 1)
                    load_expert(b, b, None if f == 0 else (f * ROUNDS - 1) * UNROLL + b * CT)
                with sp.Fori(1, ROUNDS) as r:
                    freed_results[0] = (r + (ROUNDS * f - 1)) * (16 * (UNROLL // Y_BUFS))
                    for b in range(W_BUFS):
                        load_expert(b, r * W_BUFS + b, (r + (ROUNDS * f - 1)) * UNROLL + b * CT)
                    if f == 0:
                        sp.dma_start(second[bass.ds(r * P, P), :, :], blank[:, :, :]).then_inc(s_blank, 16)
                if f == 0:
                    sp.dma_start(second[0:P, :, :], blank[:, :, :]).then_inc(s_blank, 16)

                for i in range(Y_BUFS):
                    sp.wait_ge(s_result[i], 16 * (STEPS // Y_BUFS) * (f + 1))
                back_rows = results.rearrange("(t k) c -> t k c", k=TOP_K)
                for t in range(2):
                    if f:
                        wait_alone(sp, s_added, TILES * f + t - 1)
                    sp.dma_start(back[:, t, :, :], back_rows[t * P:(t + 1) * P]).then_inc(s_back[t], 16)
                with sp.Fori(1, TILES // 2) as i:
                    for t in range(2):
                        wait_alone(sp, s_added, i * 2 + (TILES * f + t - 1))
                        sp.dma_start(back[:, t, :, :], back_rows[bass.ds((i * 2 + t) * P, P), :, :]).then_inc(s_back[t], 16)
            wait_alone(sp, s_added, TILES * FFNS)
            sp.dma_start(out.rearrange("(t p) d -> p t d", p=P), x_res[:, :, :]).then_inc(s_out, 16)
            sp.wait_ge(s_out, 16)

        @block.gpsimd
        def _(pool):
            done = Tally(s_pool)
            done.add(nc.gpsimd.memset(ident[:, :], 1.0))
            done.add(nc.gpsimd.memset(earlier[:, :], 1.0))
            done.add(nc.gpsimd.memset(ones[:, :], 1.0))
            n = done.add(nc.gpsimd.iota(slot_base[:, :], pattern=[[CAP, E]], base=1, channel_multiplier=0,
                                        allow_small_or_imprecise_dtypes=True))
            nc.gpsimd.memset(blank[:, :, :], 0.0).then_inc(s_blank_set, 1)
            pool.wait_ge(s_blank_set, 1)
            nc.gpsimd.memset(blank[:, :, D:D + 1].bitcast(I32), NOWHERE).then_inc(s_blank_set, 1)
            pool.wait_ge(s_pool, n)
            nc.gpsimd.affine_select(out=ident[:, :], in_=ident[:, :], compare_op=ALU.is_equal, fill=0.0,
                                    base=0, pattern=[[-1, P]], channel_multiplier=1).then_inc(s_const, 1)
            nc.gpsimd.affine_select(out=earlier[:, :], in_=earlier[:, :], compare_op=ALU.is_gt, fill=0.0,
                                    base=0, pattern=[[1, P]], channel_multiplier=-1).then_inc(s_const, 1)
            nc.gpsimd.iota(result_row[:, :, :], pattern=[[P * TOP_K, TILES], [1, TOP_K]], base=0,
                           channel_multiplier=TOP_K).then_inc(s_const, 1)

            for f in range(FFNS):
                pool.wait_ge(s_blank, 16 * (ROUNDS + SENT // P // BLANK_ROWS + ROUNDS * f))
                with pool.Fori(0, GROUPS) as g:
                    for j in range(GT):
                        wait_alone(pool, s_slot, g * GT + (f * TILES + j + 1))
                        for k in range(TOP_K):
                            nc.gpsimd.indirect_dma_start(
                                out=slot_rows[f], out_offset=bass.IndirectOffsetOnAxis(ap=slot_idx[:, j, k:k + 1], axis=0),
                                in_=row[:, j, k, :], in_offset=None, bounds_check=SLOTS - 1,
                                oob_is_err=False).then_inc(s_sent[j], 16)
                with pool.Fori(0, ROUNDS) as r:
                    for s in range(UNROLL):
                        b, c = s // CT, s % CT
                        wait_alone(pool, s_y, r * UNROLL + (f * STEPS + s + 1))
                        nc.gpsimd.indirect_dma_start(
                            out=results, out_offset=bass.IndirectOffsetOnAxis(
                                ap=slots_sb[:, b, c, D:D + 1].bitcast(U32), axis=0),
                            in_=y_sb[:, s % Y_BUFS, :], in_offset=None, bounds_check=SENT - 1,
                            oob_is_err=False).then_inc(s_result[s % Y_BUFS], 16)

        @block.tensor
        def _(pe):
            def mm(out_, lhsT, rhs, first, last):
                return nc.tensor.matmul(out_, lhsT, rhs, start=first, stop=last)

            def route_group(g, f):
                for j in range(GT):
                    pe.wait_ge(s_row, g * GT + (j + 1))
                    for k in range(KD):
                        t = nc.tensor.transpose(rowT_ps[k][:, j * P:(j + 1) * P],
                                                row[:, j, 0, k * P:(k + 1) * P], ident[:, :])
                t.then_inc(s_rowT, 1)
                pe.wait_ge(s_xnT, (g + 1) * KD)
                for j in range(GT):
                    for k in range(KD):
                        m = mm(logits_ps[:, j * E:(j + 1) * E], xnT[:, k, j * P:(j + 1) * P],
                               gate_sb[:, k, :], k == 0, k == KD - 1)
                m.then_inc(s_logits, 1)

            def positions(g, j, f):
                pe.wait_ge(s_mask, g * GT + (j + 1))
                pe.wait_ge(s_before, g * GT + (j + 1 + f))
                mm(pos_ps[:, j * E:(j + 1) * E], earlier[:, :], mask[:, j, :], True, False)
                mm(pos_ps[:, j * E:(j + 1) * E], ones[:, :], before[:, j, :], False, True).then_inc(s_pos, 1)

            def shared_up(g, c):
                f0, fn = FC[c]
                if c:
                    pe.wait_ge(s_shh, g * len(FC) + c)
                for k in range(KD):
                    mm(shg_ps[0:fn, :], shg_sb[:, k, f0:f0 + fn], xnT[:, k, :], k == 0, k == KD - 1)
                for k in range(KD):
                    m = mm(shu_ps[0:fn, :], shu_sb[:, k, f0:f0 + fn], xnT[:, k, :], k == 0, k == KD - 1)
                m.then_inc(s_shgu, 1)

            def shared_down(g):
                pe.wait_ge(s_shh, (g + 1) * len(FC))
                for j in range(GT):
                    if j >= 2:
                        pe.wait_ge(s_shadd, g * GT + (j - 1))
                    for c, (f0, fn) in enumerate(FC):
                        m = mm(sho_ps[j % 2][:, 0:D], sh_h[0:fn, c, j * P:(j + 1) * P], shd_sb[0:fn, c, :],
                               c == 0, c == len(FC) - 1)
                    m.then_inc(s_shout, 1)

            def ffn_in(g, f):
                route_group(g, f)
                for c in range(len(FC)):
                    positions(g, c, f)
                    shared_up(g, c)
                positions(g, GT - 1, f)
                shared_down(g)
                pe.wait_ge(s_shadd, (g + 1) * GT)
                pe.wait_ge(s_slot, (g + 1) * GT)

            def slots_T(s, at, b, c):
                if c == 0:
                    pe.wait_ge(s_slots[b], 16 * at["round"])
                if at["full"]:
                    pe.wait_ge(s_xT, at["base"] + (s - 1))
                for k in range(KD):
                    t = nc.tensor.transpose(xT_ps[s % 2][:, k * P:(k + 1) * P],
                                            slots_sb[:, b, c, k * P:(k + 1) * P], ident[:, :])
                t.then_inc(s_xT_ps, 1)

            def gate_up(s, at, b, c):
                if c == 0:
                    pe.wait_ge(s_wgu[b], 16 * at["round"])
                pe.wait_ge(s_xT, at["base"] + (s + 1))
                if at["full"]:
                    pe.wait_ge(s_h, at["base"] + (s - 1))
                for k in range(KD):
                    m = mm(gu_ps[s % 2][:, 0:2 * F], xT[:, s % 2, k, :], wgu_sb[:, b, k, :], k == 0, k == KD - 1)
                m.then_inc(s_gu, 1)

            def h_T(s, at, b, c):
                pe.wait_ge(s_h, at["base"] + (s + 1))
                if at["full"]:
                    pe.wait_ge(s_hT, at["base"] + (s - 1))
                for k in range(2):
                    t = nc.tensor.transpose(hT_ps[s % 2][0:FH, k * P:(k + 1) * P],
                                            h[:, s % 2, k * FH:(k + 1) * FH], ident[:, :])
                t.then_inc(s_hT_ps, 1)

            def down(s, at, b, c):
                if c == 0:
                    pe.wait_ge(s_wd[b], 16 * at["round"])
                pe.wait_ge(s_hT, at["base"] + (s + 1))
                if at["full"]:
                    pe.wait_ge(s_y, at["base"] + (s - 1))
                for k in range(2):
                    m = mm(y_ps[s % 2][:, 0:D], hT[:, s % 2, k, :], wd_sb[:, b, k, :], k == 0, k == 1)
                m.then_inc(s_y_ps, 1)

            STAGES = (slots_T, gate_up, h_T, down)

            def experts(f):
                pipeline(pe, f, STAGES)

            def attention(g):
                for j in range(GT):
                    pe.wait_ge(s_xa, g * GT + (j + 1))
                    for k in range(KD):
                        t = nc.tensor.transpose(bank[k][:, j * P:(j + 1) * P], xa[:, j, k * P:(k + 1) * P],
                                                ident[:, :])
                t.then_inc(s_xaT_ps, 1)
                pe.wait_ge(s_xaT, g + 1)
                for m_ in range(4):
                    for k in range(KD):
                        m = mm(bank[2 + m_][:, :], wqkv_sb[:, k, m_ * P:(m_ + 1) * P], xaT[:, k, :], k == 0, k == KD - 1)
                    m.then_inc(s_qk_ps, 1)
                for j in range(GT):
                    if j >= 2:
                        pe.wait_ge(s_v, g * GT + (j - 1))
                    for k in range(KD):
                        m = mm(bank[6 + j % 2][:, 0:D], xaT[:, k, j * P:(j + 1) * P], wqkv_sb[:, k, 2 * D:3 * D],
                               k == 0, k == KD - 1)
                    m.then_inc(s_v_ps, 1)
                pe.wait_ge(s_qk, (g + 1) * 4)
                for j in range(GT):
                    for k in range(KD):
                        m = mm(bank[2 + j][:, :], qkT[:, k, j * P:(j + 1) * P], qkT[:, KD + k, :], k == 0, k == KD - 1)
                    m.then_inc(s_score, 1)
                pe.wait_ge(s_v, (g + 1) * GT)
                tb = [bank[0], bank[1], bank[6], bank[7]]
                for j in range(GT):
                    pe.wait_ge(s_attn, g * GT + (j + 1))
                    for c in range(GT):
                        t = nc.tensor.transpose(tb[c][:, j * P:(j + 1) * P], attn[:, j, c * P:(c + 1) * P],
                                                ident[:, :])
                t.then_inc(s_attnT_ps, 1)
                for m_ in range(KD):
                    for c in range(GT):
                        if m_ == 0:
                            pe.wait_ge(s_attnT, g * GT + (c + 1))
                        m = mm(bank[2 + m_][:, :], v_sb[:, c, m_ * P:(m_ + 1) * P], attnT[:, c, :], c == 0, c == GT - 1)
                    m.then_inc(s_ctx_ps, 1)
                pe.wait_ge(s_ctx, (g + 1) * KD)
                for j in range(GT):
                    for k in range(KD):
                        m = mm(bank[4 + j][:, 0:D], ctxT[:, k, j * P:(j + 1) * P], wo_sb[:, k, :], k == 0, k == KD - 1)
                    m.then_inc(s_o_ps, 1)

            pe.wait_ge(s_const, 4)
            pe.wait_ge(s_load, 16 * LOADS)
            with pe.Fori(0, GROUPS) as g:
                ffn_in(g, 0)
            experts(0)
            pe.wait_ge(s_y, STEPS)
            with pe.Fori(0, GROUPS) as g:
                attention(g)
                ffn_in(g + GROUPS, 1)
            experts(1)

        @block.scalar
        def _(act):
            def copy(out_, in_):
                return nc.scalar.activation(out_, in_, ACT.Copy)

            def ffn_in(g):
                act.wait_ge(s_var, g + 1)
                nc.scalar.activation(std[:, :], mv[:, :, 1], ACT.Sqrt, bias=eps[:, 0:1]).then_inc(s_std, 1)
                act.wait_ge(s_rowT, g + 1)
                for k in range(KD):
                    copy(xnT[:, k, :], rowT_ps[k][:, :]).then_inc(s_xnT, 1)
                act.wait_ge(s_negmax, (g + 1) * GT)
                for j in range(GT):
                    nc.scalar.activation(expl[:, j, :], logits_ps[:, j * E:(j + 1) * E], ACT.Exp,
                                         bias=neg_max[:, j:j + 1], accum_out=expsum[:, j:j + 1]).then_inc(s_expl, 1)
                for c, (f0, fn) in enumerate(FC):
                    act.wait_ge(s_shgu, g * len(FC) + (c + 1))
                    if c:
                        act.wait_ge(s_shh, g * len(FC) + c)
                    nc.scalar.activation(sh_act[0:fn, :], shg_ps[0:fn, :], ACT.Silu).then_inc(s_shact, 1)

            def copy_slots_T(s, at, b, c):
                act.wait_ge(s_xT_ps, at["base"] + (s + 1))
                if at["full"]:
                    act.wait_ge(s_gu, at["base"] + (s - 1))
                copy(xT[:, s % 2, :, :], xT_ps[s % 2][:, 0:KD * P]).then_inc(s_xT, 1)

            def silu(s, at, b, c):
                act.wait_ge(s_gu, at["base"] + (s + 1))
                if at["full"]:
                    act.wait_ge(s_h, at["base"] + (s - 1))
                nc.scalar.activation(act_g[:, s % 2, :], gu_ps[s % 2][:, 0:F], ACT.Silu).then_inc(s_act, 1)

            def copy_y(s, at, b, c):
                act.wait_ge(s_y_ps, at["base"] + (s + 1))
                if at["y_full"]:
                    act.wait_ge(s_result[s % Y_BUFS], y_count(at, s))
                copy(y_sb[:, s % Y_BUFS, :], y_ps[s % 2][:, 0:D]).then_inc(s_y, 1)

            def y_count(at, s):
                return (at["round"] - 1) * (16 * (UNROLL // Y_BUFS)) + 16 * (s // Y_BUFS)

            def attention(g):
                act.wait_ge(s_avar, g + 1)
                nc.scalar.activation(std[:, :], mv[:, :, 1], ACT.Sqrt, bias=eps[:, 0:1]).then_inc(s_astd, 1)
                act.wait_ge(s_xaT_ps, g + 1)
                copy(xaT[:, 0, :], bank[0][:, :])
                copy(xaT[:, 1, :], bank[1][:, :]).then_inc(s_xaT, 1)
                for m_ in range(4):
                    act.wait_ge(s_qk_ps, g * 4 + (m_ + 1))
                    nc.scalar.activation(qkT[:, m_, :], bank[2 + m_][:, :], ACT.Identity,
                                         bias=bqk_sb[:, m_:m_ + 1]).then_inc(s_qk, 1)
                for j in range(GT):
                    act.wait_ge(s_rowmax, g * GT + (j + 1))
                    nc.scalar.activation(attn[:, j, :], bank[2 + j][:, :], ACT.Exp, bias=neg_row_max[:, j:j + 1],
                                         scale=float(D) ** -0.5, accum_out=attn_sum[:, j:j + 1]).then_inc(s_attn, 1)
                act.wait_ge(s_ctx_ps, g * KD + 1)
                copy(ctxT[:, 0, :], bank[2][:, :]).then_inc(s_ctx, 1)
                act.wait_ge(s_ctx_ps, g * KD + 2)
                copy(ctxT[:, 1, :], bank[3][:, :]).then_inc(s_ctx, 1)

            act.wait_ge(s_const, 4)
            act.wait_ge(s_load, 16 * LOADS)
            with act.Fori(0, GROUPS) as g:
                ffn_in(g)
            pipeline(act, 0, (copy_slots_T, silu, None, copy_y))
            with act.Fori(0, GROUPS) as g:
                attention(g)
                ffn_in(g + GROUPS)
            pipeline(act, 1, (copy_slots_T, silu, None, copy_y))

        @block.vector
        def _(dve):
            done = Tally(s_dve)

            def after(n=None, alone=False):
                (wait_alone if alone else type(dve).wait_ge)(dve, s_dve, done.at(done.n if n is None else n))

            def norm_stats(t0, signal):
                for j in range(GT):
                    n = done.add(nc.vector.bn_stats(stats[:, j, :], x_res[:, bass.ds(t0 + j, 1), :].rearrange("p a d -> p (a d)")))
                for j in range(GT):
                    after(n - GT + 1 + j, alone=True)
                    i = nc.vector.bn_aggr(mv[:, j, :], stats[:, j, :])
                    if j == GT - 1:
                        i.then_inc(signal, 1)

            def x_tile(t):
                return x_res[:, bass.ds(t, 1), :].rearrange("p a d -> p (a d)")

            def ffn_in(t0, g, sent):
                if sent is not None:
                    dve.wait_ge(s_shadd, g * GT)
                after(alone=True)
                norm_stats(t0, s_var)
                dve.wait_ge(s_std, g + 1)
                done.add(nc.vector.reciprocal(rstd[:, :], std[:, :]))
                dve.wait_ge(s_var, g + 1)
                after()
                for j in range(GT):
                    if sent is not None:
                        dve.wait_ge(s_sent[j], sent)
                    done.add(nc.vector.tensor_copy(row[:, j, :, D:D + 1].bitcast(I32),
                                          result_row[:, bass.ds(t0 + j, 1), :].rearrange("p a (k o) -> p (a k) o", o=1)))
                    nc.vector.tensor_scalar(row[:, j, :, 0:D],
                                            x_res[:, bass.ds(t0 + j, 1), :].broadcast_to([P, TOP_K, D]),
                                            mv[:, j, 0:1], rstd[:, j:j + 1], ALU.subtract, ALU.mult).then_inc(s_row, 1)
                wait_alone(dve, s_logits, g + 1)
                for j in range(GT):
                    done.add(nc.vector.max(top_logits[:, j, :], logits_ps[:, j * E:(j + 1) * E]))
                    after()
                    nc.vector.tensor_scalar(neg_max[:, j:j + 1], top_logits[:, j, 0:1], -1.0, None,
                                            ALU.mult).then_inc(s_negmax, 1)
                for j in range(GT):
                    dve.wait_ge(s_expl, g * GT + (j + 1))
                    done.add(nc.vector.reciprocal(rexpsum[:, j:j + 1], expsum[:, j:j + 1]))
                    after()
                    done.add(nc.vector.tensor_scalar(probs[:, j, 0:E], expl[:, j, :], rexpsum[:, j:j + 1], None, ALU.mult))
                    after(alone=True)
                    done.add(nc.vector.max(top[:, j, :], probs[:, j, 0:E]))
                    after()
                    done.add(nc.vector.tensor_copy(chosen[:, j, 0:TOP_K], top[:, j, 0:TOP_K]))
                    done.add(nc.vector.reduce_sum(topsum[:, j:j + 1], top[:, j, 0:TOP_K], axis=AX.X))
                    after(alone=True)
                    done.add(nc.vector.match_replace(marked[:, j, :], in_to_replace=chosen[:, j, :], in_values=probs[:, j, :], imm_value=-2.0))
                    done.add(nc.vector.tensor_scalar(topsum[:, j:j + 1], topsum[:, j:j + 1], 1e-20, None, ALU.add))
                    after()
                    nc.vector.tensor_scalar(mask[:, j, :], marked[:, j, 0:E], -2.0, None, ALU.is_equal).then_inc(s_mask, 1)
                    done.add(nc.vector.reciprocal(rtop[:, j:j + 1], topsum[:, j:j + 1]))
                    dve.wait_ge(s_mask, g * GT + (j + 1))
                    nc.vector.tensor_tensor(before[:, (j + 1) % GT, :], before[:, j, :], mask[:, j, :], ALU.add).then_inc(s_before, 1)
                    dve.wait_ge(s_pos, g * GT + (j + 1))
                    done.add(nc.vector.scalar_tensor_tensor(out=kept[:, j, :], in0=pos_ps[:, j * E:(j + 1) * E], scalar=float(CAP),
                                                            in1=mask[:, j, :], op0=ALU.is_lt, op1=ALU.mult))
                    done.add(nc.vector.tensor_tensor(key[:, j, :], pos_ps[:, j * E:(j + 1) * E], slot_base[:, :], ALU.add))
                    after()
                    done.add(nc.vector.tensor_tensor(key[:, j, :], key[:, j, :], kept[:, j, :], ALU.mult))
                    done.add(nc.vector.scalar_tensor_tensor(out=wkept[:, j, :], in0=probs[:, j, 0:E], scalar=rtop[:, j:j + 1],
                                                            in1=kept[:, j, :], op0=ALU.mult, op1=ALU.mult))
                    after(alone=True)
                    done.add(nc.vector.max(top_keys[:, j, :], key[:, j, :]))
                    after()
                    done.add(nc.vector.tensor_tensor(is_key[:, j, :, :], key[:, j, None, :].broadcast_to([P, TOP_K, E]),
                                                     top_keys[:, j, 0:TOP_K].rearrange("p (k o) -> p k o", o=1).broadcast_to([P, TOP_K, E]), ALU.is_equal))
                    done.add(nc.vector.tensor_scalar(absent[:, j, :], top_keys[:, j, 0:TOP_K], 0.0, float(NOWHERE), ALU.is_equal, ALU.mult))
                    after()
                    done.add(nc.vector.tensor_tensor(is_key[:, j, :, :], is_key[:, j, :, :], wkept[:, j, None, :].broadcast_to([P, TOP_K, E]), ALU.mult))
                    done.add(nc.vector.tensor_tensor(slot_f[:, j, :], absent[:, j, :], top_keys[:, j, 0:TOP_K], ALU.add))
                    after()
                    done.add(nc.vector.reduce_sum(w_row[:, j, :], is_key[:, j, :, :], axis=AX.X))
                    after()
                    done.add(nc.vector.tensor_scalar(w_tok[:, bass.ds(t0 + j, 1), :].rearrange("p a k -> p (a k)"),
                                                     w_row[:, j, :], 0.5, None, ALU.mult))
                    nc.vector.tensor_scalar(slot_idx[:, j, :], slot_f[:, j, :], -1.0, None, ALU.add).then_inc(s_slot, 1)
                    if j < len(FC):
                        shared_h(g, j)
                for j in range(GT):
                    dve.wait_ge(s_shout, g * GT + (j + 1))
                    nc.vector.scalar_tensor_tensor(out=x_tile(t0 + j), in0=sho_ps[j % 2][:, 0:D], scalar=0.5, in1=x_tile(t0 + j),
                                                   op0=ALU.mult, op1=ALU.add).then_inc(s_shadd, 1)

            def shared_h(g, c):
                f0, fn = FC[c]
                dve.wait_ge(s_shact, g * len(FC) + (c + 1))
                nc.vector.tensor_tensor(sh_h[0:fn, c, :], sh_act[0:fn, :], shu_ps[0:fn, :], ALU.mult).then_inc(s_shh, 1)

            def hidden(s, at, b, c):
                dve.wait_ge(s_act, at["base"] + (s + 1))
                if at["full"]:
                    dve.wait_ge(s_hT_ps, at["base"] + (s - 1))
                nc.vector.tensor_tensor(h[:, s % 2, :], act_g[:, s % 2, :], gu_ps[s % 2][:, F:2 * F], ALU.mult).then_inc(s_h, 1)

            def copy_hT(s, at, b, c):
                dve.wait_ge(s_hT_ps, at["base"] + (s + 1))
                if at["full"]:
                    dve.wait_ge(s_y_ps, at["base"] + (s - 1))
                nc.vector.tensor_copy(hT[:, s % 2, :, :], hT_ps[s % 2][0:FH, 0:2 * P]).then_inc(s_hT, 1)

            def combine(t, n, buf, in_buf):
                dve.wait_ge(s_back[buf], in_buf * 16)
                for k in range(TOP_K):
                    i = nc.vector.scalar_tensor_tensor(out=x_tile(t), in0=back[:, buf, k, :],
                                                       scalar=w_tok[:, bass.ds(t, 1), k:k + 1].rearrange("p a k -> p (a k)"), in1=x_tile(t),
                                                       op0=ALU.mult, op1=ALU.add)
                    if k < TOP_K - 1:
                        done.add(i)
                        after()
                i.then_inc(s_added, 1)

            def attention(g):
                t0 = g * GT
                for j in range(GT):
                    combine(t0 + j, 0, j % 2, g * 2 + (j // 2 + 1))
                wait_alone(dve, s_added, g * GT + GT)
                norm_stats(t0, s_avar)
                dve.wait_ge(s_astd, g + 1)
                done.add(nc.vector.reciprocal(rstd[:, :], std[:, :]))
                dve.wait_ge(s_avar, g + 1)
                after()
                for j in range(GT):
                    nc.vector.tensor_scalar(xa[:, j, :], x_tile(t0 + j), mv[:, j, 0:1], rstd[:, j:j + 1],
                                            ALU.subtract, ALU.mult).then_inc(s_xa, 1)
                for j in range(GT):
                    n_bias = done.add(nc.vector.tensor_tensor(x_tile(t0 + j), x_tile(t0 + j), bo_sb[:, :], ALU.add))
                for j in range(GT):
                    dve.wait_ge(s_v_ps, g * GT + (j + 1))
                    nc.vector.tensor_tensor(v_sb[:, j, :], bank[6 + j % 2][:, 0:D], bv_sb[:, :], ALU.add).then_inc(s_v, 1)
                for j in range(GT):
                    dve.wait_ge(s_score, g * GT + (j + 1))
                    done.add(nc.vector.reduce_max(row_max[:, j:j + 1], bank[2 + j][:, :], axis=AX.X))
                    after()
                    nc.vector.tensor_scalar(neg_row_max[:, j:j + 1], row_max[:, j:j + 1], -float(D) ** -0.5, None,
                                            ALU.mult).then_inc(s_rowmax, 1)
                dve.wait_ge(s_attn, (g + 1) * GT)
                done.add(nc.vector.reciprocal(rattn[:, :], attn_sum[:, :]))
                dve.wait_ge(s_attnT_ps, g + 1)
                tb = [bank[0], bank[1], bank[6], bank[7]]
                for c in range(GT):
                    nc.vector.tensor_copy(attnT[:, c, :], tb[c][:, :]).then_inc(s_attnT, 1)
                after()
                for j in range(GT):
                    dve.wait_ge(s_o_ps, g * GT + (j + 1))
                    done.add(nc.vector.scalar_tensor_tensor(out=x_tile(t0 + j), in0=bank[4 + j][:, 0:D], scalar=rattn[:, j:j + 1],
                                                            in1=x_tile(t0 + j), op0=ALU.mult, op1=ALU.add))
                after(alone=True)

            def start_positions():
                nc.vector.memset(before[:, 0, :], 0.0).then_inc(s_before, 1)

            nc.vector.memset(eps[:, :], EPS).then_inc(s_const, 1)
            done.add(nc.vector.memset(row[:, :, :, D:ROW], 0.0))
            done.add(nc.vector.memset(probs[:, :, E:E + 2], -1.0))
            done.add(nc.vector.memset(chosen[:, :, TOP_K:8], -1.0))
            after()
            dve.wait_ge(s_const, 4)
            dve.wait_ge(s_load, 16 * LOADS)
            dve.wait_ge(s_x, 16 * GROUPS)

            start_positions()
            first = done.n
            ffn_in(0, 0, None)
            per = done.n - first
            with dve.Fori(1, GROUPS) as g:
                done.base = (g - 1) * per
                start = done.n
                ffn_in(g * GT, g, g * (16 * TOP_K))
                assert done.n - start == per
            done.base, done.n = 0, first + per * GROUPS
            pipeline(dve, 0, (None, hidden, copy_hT, None))

            start_positions()
            first = done.n
            with dve.Fori(0, GROUPS) as g:
                done.base = g * ATT_OPS
                attention(g)
                ffn_in(g * GT, g + GROUPS, (g + GROUPS) * (16 * TOP_K))
                assert done.n - first == ATT_OPS, done.n - first
            done.base, done.n = 0, first + ATT_OPS * GROUPS
            pipeline(dve, 1, (None, hidden, copy_hT, None))

            first = done.n
            with dve.Fori(0, TILES // 2) as i:
                done.base = i * (2 * (TOP_K - 1))
                for t in range(2):
                    combine(i * 2 + t, 0, t, i + (TILES // 2 + 1))
            done.base, done.n = 0, first + TILES * (TOP_K - 1)


ATT_OPS = 127
_OUT = (B, S, D)


def kernel(L0_attn_hidden_states, L0_attn_w_qkv, L0_attn_b_qkv, L0_attn_w_out, L0_attn_b_out,
           L0_ffn_gate_w, L0_ffn_w_gate, L0_ffn_w_up, L0_ffn_w_down, L0_ffn_sh_gate, L0_ffn_sh_up, L0_ffn_sh_down):
    import concourse.bacc as bacc
    from concourse.bass_utils import run_bass_kernel_spmd

    def chunks(w, p=P):
        w = np.asarray(w).T
        return w.reshape(w.shape[0] // p, p, w.shape[1]).transpose(1, 0, 2)

    w_gu = np.concatenate([np.asarray(L0_ffn_w_gate), np.asarray(L0_ffn_w_up)], axis=1)
    w_gu = w_gu.transpose(0, 2, 1).reshape(E, KD, P, 2 * F).transpose(0, 2, 1, 3).reshape(E * P, KD, 2 * F)
    w_d = np.asarray(L0_ffn_w_down).transpose(0, 2, 1).reshape(E, 2, FH, D).transpose(0, 2, 1, 3).reshape(E * FH, 2, D)
    b = np.asarray(L0_attn_b_qkv)
    arrays = {
        "x": np.asarray(L0_attn_hidden_states).reshape(N, D),
        "wqkv": chunks(L0_attn_w_qkv),
        "woT": chunks(L0_attn_w_out),
        "bqk": b[0:2 * D].reshape(4, P).T,
        "bv": np.broadcast_to(b[2 * D:], (P, D)),
        "bo": np.broadcast_to(np.asarray(L0_attn_b_out), (P, D)),
        "gateT": chunks(L0_ffn_gate_w),
        "w_gu": w_gu,
        "w_d": w_d,
        "sh_g": chunks(L0_ffn_sh_gate),
        "sh_u": chunks(L0_ffn_sh_up),
        "sh_d": np.asarray(L0_ffn_sh_down).T,
    }
    arrays = {name: np.ascontiguousarray(a) for name, a in arrays.items()}
    nc = bacc.Bacc("TRN2", target_bir_lowering=False, num_devices=1)
    aps = {n: nc.dram_tensor(n, a.shape, mybir.dt.from_np(a.dtype), kind="ExternalInput").ap() for n, a in arrays.items()}
    out = nc.dram_tensor("out", (N, D), F32, kind="ExternalOutput").ap()
    build(nc, **aps, out=out)
    got = run_bass_kernel_spmd(nc, [arrays], core_ids=[0])
    return got.results[0]["out"].reshape(_OUT)
```

```python
from contextlib import ExitStack

import numpy as np

import concourse.bass as bass
from concourse import mybir

F32 = mybir.dt.float32
BF16 = mybir.dt.bfloat16
I32 = mybir.dt.int32
U32 = mybir.dt.uint32
ALU = mybir.AluOpType
ACT = mybir.ActivationFunctionType
AX = mybir.AxisListType

P = 128
B, S, D = 4, 512, 256
N = B * S
E, F, FS, TOP_K, CAP_FACTOR = 64, 176, 352, 6, 2
CAP = CAP_FACTOR * ((N * TOP_K + E - 1) // E)
EPS = 1e-5

KD = D // P
TILES = N // P
GROUPS = B
GT = TILES // GROUPS
FH = F // 2
CT = CAP // P
MT = 2
MAIN = MT * P
SLOTS = E * CAP
STEPS = E * MT
SENT = N * TOP_K
NOWHERE = 1 << 20
HALF_TILES = E * CT // 2
FC = [(0, 128), (128, 128), (256, FS - 256)]
FFNS = 2
W_BUFS = 4
X_BUFS = 8
Y_BUFS = 4
ROUND = 16
ROUNDS = STEPS // ROUND
ROUND_E = ROUND // MT
SCATTER_LAG = 8
BLANK_ROWS = 12
assert CAP % P == 0 and CT == MT + 1 and STEPS % ROUND == 0 and GT == 4 and KD == 2


class Tally:

    def __init__(self, sem):
        self.sem, self.base, self.n = sem, 0, 0

    def add(self, instruction):
        self.n += 1
        instruction.then_inc(self.sem, 1)
        return self.n

    def at(self, n):
        return self.base + n


def build(nc, x, wqkv, woT, bqk, bv, bo, gateT, w_gu, w_d, sh_g, sh_u, sh_d, out):
    table = [nc.dram_tensor(f"table{f}", (SLOTS, 2), F32).ap() for f in range(FFNS)]
    xn_rows = [nc.dram_tensor(f"xn_rows{f}", (N, D), F32).ap() for f in range(FFNS)]
    results = nc.dram_tensor("results", (SENT, D), F32).ap()

    with ExitStack() as ctx:
        def sb(name, shape, dt=F32):
            return ctx.enter_context(nc.sbuf_tensor(name, shape, dt))

        def sem(name):
            return ctx.enter_context(nc.semaphore(name))

        x_res = sb("x_res", [P, TILES, D])
        wqkv_sb = sb("wqkv_sb", [P, KD, 3 * D])
        wo_sb = sb("wo_sb", [P, KD, D])
        bqk_sb = sb("bqk_sb", [P, 4])
        bq_scaled = sb("bq_scaled", [P, KD])
        bv_sb = sb("bv_sb", [P, D])
        bo_sb = sb("bo_sb", [P, D])
        gate_sb = sb("gate_sb", [P, KD, E])
        shg_sb = sb("shg_sb", [P, KD, FS])
        shu_sb = sb("shu_sb", [P, KD, FS])
        shd_sb = sb("shd_sb", [P, len(FC), D])
        ident = sb("ident", [P, P])
        earlier = sb("earlier", [P, P], BF16)
        ones = sb("ones", [P, P], BF16)
        slot_base = sb("slot_base", [P, E])
        entry = sb("entry", [P, TILES, TOP_K, 2])
        zeros = sb("zeros", [P, BLANK_ROWS, D])
        blank = sb("blank", [P, SLOTS * 2 // P])
        eps = sb("eps", [P, 1])
        stats = sb("stats", [P, GT, 6])
        mv = sb("mv", [P, GT, 2])
        std = sb("std", [P, GT])
        rstd = sb("rstd", [P, GT])
        xn = sb("xn", [P, GT, D])
        xnT = sb("xnT", [P, KD, S])
        neg_max = sb("neg_max", [P, GT])
        expl = sb("expl", [P, GT, E])
        expsum = sb("expsum", [P, GT])
        rexpsum = sb("rexpsum", [P, GT])
        probs = sb("probs", [P, GT, E + 2])
        top = sb("top", [P, GT, 8])
        chosen = sb("chosen", [P, GT, 8])
        topsum = sb("topsum", [P, GT])
        rtop = sb("rtop", [P, GT])
        marked = sb("marked", [P, GT, E + 2])
        mask = sb("mask", [P, GT, E], BF16)
        mask_sum = sb("mask_sum", [P, E])
        before = sb("before", [P, E], BF16)
        kept = sb("kept", [P, GT, E])
        key = sb("key", [P, GT, E])
        wkept = sb("wkept", [P, GT, E])
        top_keys = sb("top_keys", [P, GT, 8])
        is_key = sb("is_key", [P, GT, TOP_K, E])
        w_row = sb("w_row", [P, GT, TOP_K])
        w_tok = sb("w_tok", [P, TILES, TOP_K])
        absent = sb("absent", [P, GT, TOP_K])
        slot_f = sb("slot_f", [P, GT, TOP_K])
        slot_idx = sb("slot_idx", [P, GT * TOP_K], U32)
        sent_entry = sb("sent_entry", [P, GT, TOP_K, 2])
        sent_idx = sb("sent_idx", [P, GT * TOP_K], U32)
        sh_act = sb("sh_act", [P, 2, S])
        sh_h = sb("sh_h", [P, len(FC), S])
        table_sb = sb("table_sb", [HALF_TILES, 2, 2 * P])
        idx = sb("idx", [P, 2, E * CT], U32)
        gather_idx = sb("gather_idx", [P, ROUND_E * CT], U32)
        scatter_idx = sb("scatter_idx", [P, ROUND_E * CT], U32)
        expert_id = sb("expert_id", [P, E])
        is_over = sb("is_over", [P, E])
        n_over = sb("n_over", [P, 1])
        n_over_i = sb("n_over_i", [P, 1], I32)
        over_key = sb("over_key", [P, 2, E])
        over_sorted = sb("over_sorted", [P, E])
        over_int = sb("over_int", [P, E], I32)
        over_list = sb("over_list", [P, E], I32)
        wgu_sb = sb("wgu_sb", [P, W_BUFS, KD, 2 * F])
        wd_sb = sb("wd_sb", [FH, W_BUFS, 2, D])
        x_sb = sb("x_sb", [P, X_BUFS, D])
        xT = sb("xT", [P, 2, KD, P])
        act_g = sb("act_g", [P, 2, F])
        h = sb("h", [P, 2, F])
        hT = sb("hT", [FH, 2, 2, P])
        y_sb = sb("y_sb", [P, Y_BUFS, D])
        over_idx = sb("over_idx", [P, 2, W_BUFS], U32)
        back = sb("back", [P, GT, TOP_K, D])
        astats = sb("astats", [P, GT, 6])
        amv = sb("amv", [P, GT, 2])
        astd = sb("astd", [P, GT])
        arstd = sb("arstd", [P, GT])
        xa = sb("xa", [P, GT, D])
        xaT = sb("xaT", [P, KD, S])
        qkT = sb("qkT", [P, 4, S])
        v_sb = sb("v_sb", [P, GT, D])
        neg_row_max = sb("neg_row_max", [P, GT])
        attn = sb("attn", [P, GT, S])
        attn_sum = sb("attn_sum", [P, GT])
        rattn = sb("rattn", [P, GT])
        attnT = sb("attnT", [P, GT, S])
        ctxT = sb("ctxT", [P, KD, S])

        bank = [ctx.enter_context(nc.psum_tensor(f"bank{i}", [P, 512], F32)) for i in range(8)]

        s_x0, s_x = sem("s_x0"), sem("s_x")
        s_load = sem("s_load")
        s_load_attn = sem("s_load_attn")
        s_zeros = sem("s_zeros")
        s_blank = sem("s_blank")
        s_blank_res = sem("s_blank_res")
        s_const = sem("s_const")
        s_bq = sem("s_bq")
        s_pool = sem("s_pool")
        s_dve = sem("s_dve")
        s_var, s_std, s_xn, s_xn_stored = sem("s_var"), sem("s_std"), sem("s_xn"), sem("s_xn_stored")
        s_xnT_ps, s_xnT, s_logits, s_negmax = sem("s_xnT_ps"), sem("s_xnT"), sem("s_logits"), sem("s_negmax")
        s_expl, s_mask, s_before, s_pos = sem("s_expl"), sem("s_mask"), sem("s_before"), sem("s_pos")
        s_slot, s_slot_taken, s_sent = sem("s_slot"), sem("s_slot_taken"), sem("s_sent")
        s_entry = sem("s_entry")
        s_shgu, s_shact, s_shh = sem("s_shgu"), sem("s_shact"), sem("s_shh")
        s_shout, s_shadd = sem("s_shout"), sem("s_shadd")
        s_table, s_table_ps, s_idx = sem("s_table"), sem("s_table_ps"), sem("s_idx")
        s_count_ps, s_over_known = sem("s_count_ps"), sem("s_over_known")
        s_wgu = [sem(f"s_wgu{i}") for i in range(W_BUFS)]
        s_wd = [sem(f"s_wd{i}") for i in range(W_BUFS)]
        s_gathered = [sem(f"s_gathered{i}") for i in range(X_BUFS)]
        s_result = [sem(f"s_result{i}") for i in range(Y_BUFS)]
        s_xT_ps, s_xT, s_gu, s_act, s_h = sem("s_xT_ps"), sem("s_xT"), sem("s_gu"), sem("s_act"), sem("s_h")
        s_hT_ps, s_hT, s_y_ps, s_y = sem("s_hT_ps"), sem("s_hT"), sem("s_y_ps"), sem("s_y")
        s_over = [{n: sem(f"s_over_{n}{f}") for n in
                   ("w", "idx", "x", "xT_ps", "xT", "gu", "act", "h", "hT_ps", "hT", "y_ps", "y", "result")}
                  for f in range(FFNS)]
        s_windows = sem("s_windows")
        s_experts_done = sem("s_experts_done")
        s_back = [sem(f"s_back{i}") for i in range(GT)]
        s_added, s_avar, s_astd, s_xa = sem("s_added"), sem("s_avar"), sem("s_astd"), sem("s_xa")
        s_xaT_ps, s_xaT, s_qk_ps, s_qk = sem("s_xaT_ps"), sem("s_xaT"), sem("s_qk_ps"), sem("s_qk")
        s_v_ps, s_v, s_score, s_rowmax, s_attn = sem("s_v_ps"), sem("s_v"), sem("s_score"), sem("s_rowmax"), sem("s_attn")
        s_attnT_ps, s_attnT, s_ctx_ps, s_ctx = sem("s_attnT_ps"), sem("s_attnT"), sem("s_ctx_ps"), sem("s_ctx")
        s_o_ps, s_projected = sem("s_o_ps"), sem("s_projected")
        s_out = sem("s_out")
        block = ctx.enter_context(nc.Block())

        f_bank, a_bank = bank[0:4], bank[4:8]
        xnT_ps = f_bank[0:2]
        logits_ps = pos_ps = f_bank[2]
        sho_ps = f_bank[2:4]

        def shgu_ps(c, attending):
            return f_bank[0:2] if attending or c != 1 else a_bank[0:2]

        xT_ps, gu_ps, hT_ps, y_ps = bank[0:2], bank[2:4], bank[4:6], bank[6:8]

        LOADS = 7
        LOADS_ATTN = 4
        CONSTS = 8
        BLANKS = SENT // P // BLANK_ROWS

        def wait_alone(eng, sem_, value):
            eng.wait_ge(sem_, value)
            eng.nop(nofuse=True)

        main = {"xT_ps": s_xT_ps, "xT": s_xT, "gu": s_gu, "act": s_act, "h": s_h, "hT_ps": s_hT_ps,
                "hT": s_hT, "y_ps": s_y_ps, "y": s_y}

        def pipeline(eng, f, stages, round_start=None):
            def turn(s, at_of):
                for i, stage in stages.items():
                    at = at_of(s - i)
                    if at is not None:
                        t = (s - i) % ROUND
                        stage(main, t, at, t // MT % W_BUFS, t % MT)

            def peeled(t):
                if not 0 <= t < STEPS:
                    return None
                return {"base": f * STEPS + t // ROUND * ROUND, "round": f * ROUNDS + t // ROUND,
                        "tile": t, "over": False, "reused": lambda bufs: f > 0 or t >= bufs}

            for s in range(ROUND):
                turn(s, peeled)
            with eng.Fori(1, ROUNDS) as r:
                if round_start is not None:
                    round_start(r)
                for s in range(ROUND):
                    def looped(t):
                        back_one = 1 if t < 0 else 0
                        return {"base": r * ROUND + (f * STEPS - ROUND * back_one),
                                "round": r + (f * ROUNDS - back_one),
                                "tile": None, "over": False, "reused": lambda bufs: True}
                    turn(s, looped)
            for s in range(STEPS, STEPS + max(stages)):
                turn(s, peeled)

        def dma_count(at, t, bufs):
            return at["round"] * (16 * (ROUND // bufs)) + 16 * (t // bufs + 1)

        def over_rounds(eng, f, body):
            eng.wait_ge(s_over_known, f + 1)
            n = eng.value_load(n_over_i[0:1, 0:1], min_val=0, max_val=E)
            with eng.Fori(0, E // W_BUFS) as q:
                with eng.If(n > q * W_BUFS):
                    body(q)

        def over_pipeline(eng, o, q, stages):
            at = {"base": q * W_BUFS, "round": None, "tile": None, "over": True}
            for turn in range(W_BUFS + max(stages)):
                for i, stage in stages.items():
                    s = turn - i
                    if 0 <= s < W_BUFS:
                        stage(o, s, dict(at, reused=lambda bufs, s=s: s >= bufs), s, 0)

        @block.sync
        def _(sp):
            def load_x(g0, g1, s_):
                sp.dma_start(x_res[:, g0 * GT:g1 * GT, :],
                             x[g0 * S:g1 * S, :].rearrange("(t p) d -> p t d", p=P)).then_inc(s_, 16)
            load_x(0, 1, s_x0)
            for dst, src in ((gate_sb, gateT), (shg_sb, sh_g), (shu_sb, sh_u)):
                sp.dma_start(dst[:, :, :], src).then_inc(s_load, 16)
            for c, (f0, fn) in enumerate(FC):
                sp.dma_start(shd_sb[0:fn, c, :], sh_d[f0:f0 + fn, :]).then_inc(s_load, 16)
            sp.dma_start(bqk_sb[:, :], bqk).then_inc(s_load, 16)
            sp.wait_ge(s_zeros, 1)
            for f in range(FFNS):
                sp.dma_start(table[f].rearrange("(p n) c -> p (n c)", p=P), blank[:, :]).then_inc(s_blank, 16)
            load_x(1, GROUPS, s_x)
            for dst, src in ((wqkv_sb, wqkv), (wo_sb, woT)):
                sp.dma_start(dst[:, :, :], src).then_inc(s_load_attn, 16)
            for dst, src in ((bv_sb, bv), (bo_sb, bo)):
                sp.dma_start(dst[:, :], src).then_inc(s_load_attn, 16)
            sp.wait_ge(s_zeros, 2)
            res = results.rearrange("(r p n) c -> r p n c", p=P, n=BLANK_ROWS)
            for r in range(BLANKS):
                sp.dma_start(res[r], zeros[:, :, :]).then_inc(s_blank_res, 16)

            def store_xn(f, g, g_all):
                wait_alone(sp, s_xn, g_all * GT + GT)
                sp.dma_start(xn_rows[f].rearrange("(t p) d -> p t d", p=P)[:, bass.ds(g * GT, GT), :],
                             xn[:, :, :]).then_inc(s_xn_stored, 16)

            def load_expert(b, e, used):
                if used is not None:
                    wait_alone(sp, s_gu, used)
                sp.dma_start(wgu_sb[:, b, :, :], w_gu[bass.ds(e * P, P), :, :]).then_inc(s_wgu[b], 16)
                if used is not None:
                    wait_alone(sp, s_y_ps, used)
                sp.dma_start(wd_sb[:, b, :, :], w_d[bass.ds(e * FH, FH), :, :]).then_inc(s_wd[b], 16)

            def load_experts(f):
                for e in range(ROUND_E):
                    load_expert(e % W_BUFS, e, None if f == 0 and e < W_BUFS else
                                f * STEPS + (e - W_BUFS + 1) * MT)
                with sp.Fori(1, ROUNDS) as r:
                    for e in range(ROUND_E):
                        load_expert(e % W_BUFS, r * ROUND_E + e, r * ROUND + (f * STEPS + (e - W_BUFS + 1) * MT))

            def over(o):
                def body(q):
                    for b in range(W_BUFS):
                        e = sp.value_load(over_list[0:1, bass.ds(q * W_BUFS + b, 1)], min_val=0, max_val=E - 1)
                        sp.dma_start(wgu_sb[:, b, :, :], w_gu[bass.ds(e * P, P), :, :]).then_inc(o["w"], 16)
                        sp.dma_start(wd_sb[:, b, :, :], w_d[bass.ds(e * FH, FH), :, :]).then_inc(o["w"], 16)
                    wait_alone(sp, o["y"], q * W_BUFS + W_BUFS)
                return body

            def load_table(f):
                sp.wait_ge(s_sent, 16 * GT * TOP_K * GROUPS * (f + 1))
                sp.dma_start(table_sb[:, :, :], table[f].rearrange("(h t s) c -> t h (s c)", h=2, s=P)).then_inc(s_table, 16)

            back_rows = results.rearrange("(t k) c -> t k c", k=TOP_K)

            def load_back(g, f):
                for j in range(GT):
                    if g is not None:
                        wait_alone(sp, s_added, g * GT + (f * TILES + j + 1 - GT))
                    elif f:
                        sp.wait_ge(s_added, f * TILES + j + 1 - GT)
                    rows = back_rows[j * P:(j + 1) * P] if g is None else back_rows[bass.ds(g * S + j * P, P), :, :]
                    sp.dma_start(back[:, j, :, :], rows).then_inc(s_back[j], 16)

            with sp.Fori(0, GROUPS) as g:
                store_xn(0, g, g)
            for f in range(FFNS):
                load_table(f)
                load_experts(f)
                sp.wait_ge(s_y_ps, STEPS * (f + 1))
                over_rounds(sp, f, over(s_over[f]))
                for i in range(Y_BUFS):
                    sp.wait_ge(s_result[i], 16 * (STEPS // Y_BUFS) * (f + 1))
                sp.wait_ge(s_experts_done, f + 1)
                load_back(None, f)
                if f == 0:
                    load_back(1, f)
                    with sp.Fori(2, GROUPS) as g:
                        load_back(g, f)
                        store_xn(1, g - 2, g + (GROUPS - 2))
                    for g in range(GROUPS - 2, GROUPS):
                        store_xn(1, g, GROUPS + g)
                else:
                    with sp.Fori(1, GROUPS) as g:
                        load_back(g, f)

        @block.gpsimd
        def _(pool):
            done = Tally(s_pool)
            nc.gpsimd.iota(entry[:, :, :, 0], pattern=[[P, TILES], [0, TOP_K]], base=0,
                           channel_multiplier=1, allow_small_or_imprecise_dtypes=True).then_inc(s_const, 1)
            nc.gpsimd.iota(entry[:, :, :, 1], pattern=[[P * TOP_K, TILES], [1, TOP_K]], base=0,
                           channel_multiplier=TOP_K, allow_small_or_imprecise_dtypes=True).then_inc(s_const, 1)
            done.add(nc.gpsimd.memset(ident[:, :], 1.0))
            n = done.add(nc.gpsimd.memset(earlier[:, :], 1.0))
            nc.gpsimd.memset(ones[:, :], 1.0).then_inc(s_const, 1)
            nc.gpsimd.iota(slot_base[:, :], pattern=[[CAP, E]], base=1, channel_multiplier=0,
                           allow_small_or_imprecise_dtypes=True).then_inc(s_const, 1)
            nc.gpsimd.iota(expert_id[:, :], pattern=[[1, E]], base=0, channel_multiplier=0,
                           allow_small_or_imprecise_dtypes=True).then_inc(s_const, 1)
            pool.wait_ge(s_pool, n)
            nc.gpsimd.affine_select(out=ident[:, :], in_=ident[:, :], compare_op=ALU.is_equal, fill=0.0,
                                    base=0, pattern=[[-1, P]], channel_multiplier=1).then_inc(s_const, 1)
            nc.gpsimd.affine_select(out=earlier[:, :], in_=earlier[:, :], compare_op=ALU.is_gt, fill=0.0,
                                    base=0, pattern=[[1, P]], channel_multiplier=-1).then_inc(s_const, 1)
            nc.gpsimd.memset(x_sb[:, :, :], 0.0).then_inc(s_pool, 1)
            n += 1
            pool.wait_ge(s_pool, n)
            done.n = n
            pool.wait_ge(s_const, CONSTS)

            def send(f, g, g_all, first=False):
                pool.wait_ge(s_slot, g_all + 1)
                if not first:
                    wait_alone(pool, s_sent, g_all * (16 * GT * TOP_K))
                nc.gpsimd.tensor_copy(sent_idx[:, :], slot_idx[:, :]).then_inc(s_slot_taken, 1)
                nc.gpsimd.tensor_copy(sent_entry[:, :, :, :], entry[:, bass.ds(g * GT, GT), :, :]).then_inc(s_entry, 1)
                wait_alone(pool, s_entry, g_all + 1)
                for j in range(GT):
                    for k in range(TOP_K):
                        n_ = j * TOP_K + k
                        nc.gpsimd.indirect_dma_start(
                            out=table[f], out_offset=bass.IndirectOffsetOnAxis(ap=sent_idx[:, n_:n_ + 1], axis=0),
                            in_=sent_entry[:, j, k, :], in_offset=None, bounds_check=SLOTS - 1,
                            oob_is_err=False).then_inc(s_sent, 16)

            def gather_rows(f, dst, idx_, sem_):
                nc.gpsimd.indirect_dma_start(
                    out=dst, out_offset=None, in_=xn_rows[f], in_offset=bass.IndirectOffsetOnAxis(ap=idx_, axis=0),
                    bounds_check=N - 1, oob_is_err=False).then_inc(sem_, 16)

            def scatter_rows(src, idx_, sem_):
                nc.gpsimd.indirect_dma_start(
                    out=results, out_offset=bass.IndirectOffsetOnAxis(ap=idx_, axis=0), in_=src, in_offset=None,
                    bounds_check=SENT - 1, oob_is_err=False).then_inc(sem_, 16)

            def column(s):
                return s // MT * CT + s % MT

            def gather(f):
                def stage(o, s, at, b, c):
                    if at["reused"](X_BUFS):
                        wait_alone(pool, o["xT_ps"], at["base"] + (s + 1 - X_BUFS))
                    i = gather_idx[:, column(s):column(s) + 1] if at["tile"] is None else idx[:, 0, column(at["tile"]):column(at["tile"]) + 1]
                    gather_rows(f, x_sb[:, s % X_BUFS, :], i, s_gathered[s % X_BUFS])
                return stage

            def scatter(o, s, at, b, c):
                wait_alone(pool, o["y"], at["base"] + (s + 1))
                w = (s + SCATTER_LAG) % ROUND
                i = scatter_idx[:, column(w):column(w) + 1] if at["tile"] is None else idx[:, 1, column(at["tile"]):column(at["tile"]) + 1]
                scatter_rows(y_sb[:, s % Y_BUFS, :], i, s_result[s % Y_BUFS])

            def experts(f):
                def round_start(r):
                    lag = SCATTER_LAG // MT * CT
                    for s_ in s_gathered:
                        pool.wait_ge(s_, (r + f * ROUNDS) * (16 * ROUND // X_BUFS))
                    for s_ in s_result:
                        wait_alone(pool, s_, r * (16 * ROUND // Y_BUFS) + (f * STEPS - SCATTER_LAG) * 16 // Y_BUFS)
                    nc.gpsimd.tensor_copy(gather_idx[:, :], idx[:, 0, bass.ds(r * (ROUND_E * CT), ROUND_E * CT)])
                    nc.gpsimd.tensor_copy(scatter_idx[:, :], idx[:, 1, bass.ds(r * (ROUND_E * CT) - lag, ROUND_E * CT)]).then_inc(s_windows, 1)
                    wait_alone(pool, s_windows, r + f * (ROUNDS - 1))
                pool.wait_ge(s_idx, f + 1)
                pool.wait_ge(s_xn_stored, 16 * GROUPS * (f + 1))
                pool.wait_ge(s_blank_res, 16 * BLANKS)
                pipeline(pool, f, {0: gather(f), SCATTER_LAG: scatter}, round_start)
                over_rounds(pool, f, over(f, s_over[f]))
                pool.sem_inc(s_experts_done, 1)

            def over(f, o):
                def body(q):
                    for b in range(W_BUFS):
                        e = pool.value_load(over_list[0:1, bass.ds(q * W_BUFS + b, 1)], min_val=0, max_val=E - 1)
                        nc.gpsimd.tensor_copy(over_idx[:, :, b:b + 1],
                                              idx[:, :, bass.ds(e * CT + MT, 1)]).then_inc(o["idx"], 1)
                    wait_alone(pool, o["idx"], q * W_BUFS + W_BUFS)
                    for b in range(W_BUFS):
                        gather_rows(f, x_sb[:, b, :], over_idx[:, 0, b:b + 1], o["x"])
                    for b in range(W_BUFS):
                        wait_alone(pool, o["y"], q * W_BUFS + (b + 1))
                        scatter_rows(y_sb[:, b, :], over_idx[:, 1, b:b + 1], o["result"])
                    wait_alone(pool, o["x"], (q + 1) * (16 * W_BUFS))
                    wait_alone(pool, o["result"], (q + 1) * (16 * W_BUFS))
                return body

            pool.wait_ge(s_blank, 16 * FFNS)
            send(0, 0, 0, first=True)
            with pool.Fori(1, GROUPS) as g:
                send(0, g, g)
            experts(0)
            with pool.Fori(0, GROUPS) as g:
                send(1, g, g + GROUPS)
            experts(1)

        @block.tensor
        def _(pe):
            def mm(out_, lhsT, rhs, first, last):
                return nc.tensor.matmul(out_, lhsT, rhs, start=first, stop=last)

            def turn_tiles(dst, src):
                for j in range(GT):
                    for k in range(KD):
                        t = nc.tensor.transpose(dst[k][:, j * P:(j + 1) * P], src[:, j, k * P:(k + 1) * P], ident[:, :])
                return t

            def norms_T(dst, src, s_src, n, s_dst):
                pe.wait_ge(s_src, n)
                turn_tiles(dst, src).then_inc(s_dst, 1)

            def logits(g):
                pe.wait_ge(s_xnT, (g + 1) * KD)
                for j in range(GT):
                    for k in range(KD):
                        m = mm(logits_ps[:, j * E:(j + 1) * E], xnT[:, k, j * P:(j + 1) * P], gate_sb[:, k, :],
                               k == 0, k == KD - 1)
                m.then_inc(s_logits, 1)

            def ffn_in(g, f):
                norms_T(xnT_ps, xn, s_xn, (g + 1) * GT, s_xnT_ps)
                logits(g)
                shared_up(g, 0, False)
                positions(g, f)
                shared_up(g, 1, False)
                shared_up(g, 2, False)
                shared_down(g)

            def positions(g, f):
                pe.wait_ge(s_mask, g + 1)
                pe.wait_ge(s_before, g + (1 + f))
                for j in range(GT):
                    dst = pos_ps[:, j * E:(j + 1) * E]
                    mm(dst, earlier[:, :], mask[:, j, :], True, False)
                    for i in range(j):
                        mm(dst, ones[:, :], mask[:, i, :], False, False)
                    m = mm(dst, ones[:, :], before[:, :], False, True)
                m.then_inc(s_pos, 1)

            def shared_up(g, c, attending):
                f0, fn = FC[c]
                shg_ps, shu_ps = shgu_ps(c, attending)
                if attending and c:
                    pe.wait_ge(s_shh, g * len(FC) + c)
                elif c == 2:
                    pe.wait_ge(s_shh, g * len(FC) + 1)
                for k in range(KD):
                    mm(shg_ps[0:fn, :], shg_sb[:, k, f0:f0 + fn], xnT[:, k, :], k == 0, k == KD - 1)
                for k in range(KD):
                    m = mm(shu_ps[0:fn, :], shu_sb[:, k, f0:f0 + fn], xnT[:, k, :], k == 0, k == KD - 1)
                m.then_inc(s_shgu, 1)

            def shared_down(g):
                pe.wait_ge(s_shh, (g + 1) * len(FC))
                for j in range(GT):
                    if j >= 2:
                        pe.wait_ge(s_shadd, g * GT + (j - 1))
                    for c, (f0, fn) in enumerate(FC):
                        m = mm(sho_ps[j % 2][:, 0:D], sh_h[0:fn, c, j * P:(j + 1) * P], shd_sb[0:fn, c, :],
                               c == 0, c == len(FC) - 1)
                    m.then_inc(s_shout, 1)

            def slots_T(o, s, at, b, c):
                if at["over"]:
                    pe.wait_ge(o["x"], at["base"] * 16 + 16 * W_BUFS)
                else:
                    pe.wait_ge(s_gathered[s % X_BUFS], dma_count(at, s, X_BUFS))
                if at["reused"](2):
                    pe.wait_ge(o["xT"], at["base"] + (s - 1))
                for k in range(KD):
                    t = nc.tensor.transpose(xT_ps[s % 2][:, k * P:(k + 1) * P],
                                            x_sb[:, s % X_BUFS, k * P:(k + 1) * P], ident[:, :])
                t.then_inc(o["xT_ps"], 1)

            def gate_up(o, s, at, b, c):
                if at["over"]:
                    pe.wait_ge(o["w"], at["base"] * 32 + 32 * W_BUFS)
                elif c == 0:
                    pe.wait_ge(s_wgu[b], dma_count(at, s, W_BUFS * MT))
                pe.wait_ge(o["xT"], at["base"] + (s + 1))
                if at["reused"](2):
                    pe.wait_ge(o["h"], at["base"] + (s - 1))
                for k in range(KD):
                    m = mm(gu_ps[s % 2][:, 0:2 * F], xT[:, s % 2, k, :], wgu_sb[:, b, k, :], k == 0, k == KD - 1)
                m.then_inc(o["gu"], 1)

            def h_T(o, s, at, b, c):
                pe.wait_ge(o["h"], at["base"] + (s + 1))
                if at["reused"](2):
                    pe.wait_ge(o["hT"], at["base"] + (s - 1))
                for k in range(2):
                    t = nc.tensor.transpose(hT_ps[s % 2][0:FH, k * P:(k + 1) * P],
                                            h[:, s % 2, k * FH:(k + 1) * FH], ident[:, :])
                t.then_inc(o["hT_ps"], 1)

            def down(o, s, at, b, c):
                if c == 0 and not at["over"]:
                    pe.wait_ge(s_wd[b], dma_count(at, s, W_BUFS * MT))
                pe.wait_ge(o["hT"], at["base"] + (s + 1))
                if at["reused"](2):
                    pe.wait_ge(o["y"], at["base"] + (s - 1))
                for k in range(2):
                    m = mm(y_ps[s % 2][:, 0:D], hT[:, s % 2, k, :], wd_sb[:, b, k, :], k == 0, k == 1)
                m.then_inc(o["y_ps"], 1)

            def over(o):
                def body(q):
                    over_pipeline(pe, o, q, {0: slots_T, 1: gate_up, 2: h_T, 3: down})
                    wait_alone(pe, o["y"], (q + 1) * W_BUFS)
                return body

            def experts(f):
                pe.wait_ge(s_shadd, TILES * (f + 1))
                pe.wait_ge(s_before, GROUPS * (f + 1) + f + 1)
                mm(a_bank[0][:, 0:E], ones[:, :], before[:, :], True, True).then_inc(s_count_ps, 1)
                pe.wait_ge(s_table, 16 * (f + 1))
                for w in range(2):
                    for half in range(2):
                        at = (w * 2 + half) * HALF_TILES
                        t = nc.tensor.transpose(bank[0][:, at:at + HALF_TILES],
                                                table_sb[:, half, w:2 * P:2], ident[0:HALF_TILES, 0:HALF_TILES])
                t.then_inc(s_table_ps, 1)
                pe.wait_ge(s_idx, f + 1)
                pe.wait_ge(s_over_known, f + 1)
                pipeline(pe, f, {0: slots_T, 1: gate_up, 2: h_T, 3: down})
                pe.wait_ge(s_y, STEPS * (f + 1))
                over_rounds(pe, f, over(s_over[f]))

            def qkv(g):
                pe.wait_ge(s_xaT, (g + 1) * KD)
                for m_ in range(4):
                    for k in range(KD):
                        m = mm(a_bank[(2 + m_) % 4][:, :], wqkv_sb[:, k, m_ * P:(m_ + 1) * P], xaT[:, k, :], k == 0, k == KD - 1)
                    m.then_inc(s_qk_ps, 1)
                for j in range(GT):
                    pe.wait_ge(s_qk, g * 4 + (j + 1))
                    for k in range(KD):
                        m = mm(a_bank[(2 + j) % 4][:, 0:D], xaT[:, k, j * P:(j + 1) * P], wqkv_sb[:, k, 2 * D:3 * D],
                               k == 0, k == KD - 1)
                    m.then_inc(s_v_ps, 1)

            def scores(g):
                for j in range(GT):
                    pe.wait_ge(s_v, g * GT + (j + 1))
                    for k in range(KD):
                        m = mm(a_bank[(2 + j) % 4][:, :], qkT[:, k, j * P:(j + 1) * P], qkT[:, KD + k, :], k == 0, k == KD - 1)
                    m.then_inc(s_score, 1)

            def probs_T(g):
                pe.wait_ge(s_attn, (g + 1) * GT)
                for j in range(GT):
                    for c in range(GT):
                        t = nc.tensor.transpose(a_bank[c][:, j * P:(j + 1) * P], attn[:, j, c * P:(c + 1) * P],
                                                ident[:, :])
                t.then_inc(s_attnT_ps, 1)

            def context(g):
                for m_ in range(KD):
                    for c in range(GT):
                        if m_ == 0:
                            pe.wait_ge(s_attnT, g * GT + (c + 1))
                        m = mm(a_bank[m_][:, :], v_sb[:, c, m_ * P:(m_ + 1) * P], attnT[:, c, :], c == 0, c == GT - 1)
                    m.then_inc(s_ctx_ps, 1)

            def project(g):
                pe.wait_ge(s_ctx, (g + 1) * KD)
                for j in range(GT):
                    for k in range(KD):
                        m = mm(a_bank[(2 + j) % 4][:, 0:D], ctxT[:, k, j * P:(j + 1) * P], wo_sb[:, k, :], k == 0, k == KD - 1)
                    m.then_inc(s_o_ps, 1)

            def sequence(a, g):
                if a is not None:
                    if g is not None:
                        pe.wait_ge(s_projected, a)
                    norms_T(a_bank[0:2], xa, s_xa, (a + 1) * GT, s_xaT_ps)
                if g is not None:
                    norms_T(xnT_ps, xn, s_xn, (g + 1) * GT, s_xnT_ps)
                if a is not None:
                    qkv(a)
                if g is not None:
                    logits(g)
                if a is not None:
                    scores(a)
                if g is not None:
                    shared_up(g, 0, True)
                    positions(g, 1)
                if a is not None:
                    probs_T(a)
                if g is not None:
                    shared_up(g, 1, True)
                if a is not None:
                    context(a)
                if g is not None:
                    shared_up(g, 2, True)
                if a is not None:
                    project(a)
                if g is not None:
                    shared_down(g)

            pe.wait_ge(s_const, CONSTS)
            pe.wait_ge(s_load, 16 * LOADS)
            with pe.Fori(0, GROUPS) as g:
                ffn_in(g, 0)
            experts(0)
            pe.wait_ge(s_load_attn, 16 * LOADS_ATTN)
            sequence(0, None)
            with pe.Fori(1, GROUPS) as g:
                sequence(g, g + (GROUPS - 1))
            sequence(None, 2 * GROUPS - 1)
            experts(1)

        @block.scalar
        def _(act):
            def copy(out_, in_):
                return nc.scalar.activation(out_, in_, ACT.Copy)

            def root(s_var_, s_std_, g, mv_, std_):
                act.wait_ge(s_var_, g + 1)
                nc.scalar.activation(std_[:, :], mv_[:, :, 1], ACT.Sqrt, bias=eps[:, 0:1]).then_inc(s_std_, 1)

            def copy_T(dst, src, s_src, s_dst, g):
                act.wait_ge(s_src, g + 1)
                for k in range(KD):
                    copy(dst[:, k, :], src[k][:, :]).then_inc(s_dst, 1)

            def exp_logits(g):
                act.wait_ge(s_negmax, g + 1)
                for j in range(GT):
                    e = nc.scalar.activation(expl[:, j, :], logits_ps[:, j * E:(j + 1) * E], ACT.Exp,
                                             bias=neg_max[:, j:j + 1], accum_out=expsum[:, j:j + 1])
                e.then_inc(s_expl, 1)

            def shared_silu(g, c, attending):
                fn = FC[c][1]
                act.wait_ge(s_shgu, g * len(FC) + (c + 1))
                if c == 2:
                    act.wait_ge(s_shh, g * len(FC) + 1)
                nc.scalar.activation(sh_act[0:fn, c % 2, :], shgu_ps(c, attending)[0][0:fn, :], ACT.Silu).then_inc(s_shact, 1)

            def ffn_in(g):
                root(s_var, s_std, g, mv, std)
                copy_T(xnT, xnT_ps, s_xnT_ps, s_xnT, g)
                exp_logits(g)
                for c in range(len(FC)):
                    shared_silu(g, c, False)

            def copy_slots_T(o, s, at, b, c):
                act.wait_ge(o["xT_ps"], at["base"] + (s + 1))
                if at["reused"](2):
                    act.wait_ge(o["gu"], at["base"] + (s - 1))
                copy(xT[:, s % 2, :, :], xT_ps[s % 2][:, 0:KD * P]).then_inc(o["xT"], 1)

            def silu(o, s, at, b, c):
                act.wait_ge(o["gu"], at["base"] + (s + 1))
                if at["reused"](2):
                    act.wait_ge(o["h"], at["base"] + (s - 1))
                nc.scalar.activation(act_g[:, s % 2, :], gu_ps[s % 2][:, 0:F], ACT.Silu).then_inc(o["act"], 1)

            def copy_y(o, s, at, b, c):
                act.wait_ge(o["y_ps"], at["base"] + (s + 1))
                if at["reused"](Y_BUFS):
                    act.wait_ge(s_result[s % Y_BUFS], dma_count(at, s - Y_BUFS, Y_BUFS))
                copy(y_sb[:, s % Y_BUFS, :], y_ps[s % 2][:, 0:D]).then_inc(o["y"], 1)

            def over(o):
                def body(q):
                    over_pipeline(act, o, q, {0: copy_slots_T, 1: silu, 3: copy_y})
                    wait_alone(act, o["result"], (q + 1) * (16 * W_BUFS))
                return body

            def experts(f):
                pipeline(act, f, {0: copy_slots_T, 1: silu, 3: copy_y})
                for s_ in s_result:
                    act.wait_ge(s_, 16 * (STEPS // Y_BUFS) * (f + 1))
                over_rounds(act, f, over(s_over[f]))

            def copy_qk(g):
                for m_ in range(4):
                    act.wait_ge(s_qk_ps, g * 4 + (m_ + 1))
                    nc.scalar.activation(qkT[:, m_, :], a_bank[(2 + m_) % 4][:, :], ACT.Identity,
                                         bias=bq_scaled[:, m_:m_ + 1] if m_ < KD else bqk_sb[:, m_:m_ + 1],
                                         scale=float(D) ** -0.5 if m_ < KD else 1.0).then_inc(s_qk, 1)

            def exp_scores(g):
                for j in range(GT):
                    act.wait_ge(s_rowmax, g * GT + (j + 1))
                    nc.scalar.activation(attn[:, j, :], a_bank[(2 + j) % 4][:, :], ACT.Exp, bias=neg_row_max[:, j:j + 1],
                                         accum_out=attn_sum[:, j:j + 1]).then_inc(s_attn, 1)

            def copy_probs_T(g):
                act.wait_ge(s_attnT_ps, g + 1)
                for c in range(GT):
                    copy(attnT[:, c, :], a_bank[c][:, :]).then_inc(s_attnT, 1)

            def copy_context(g):
                for k in range(KD):
                    act.wait_ge(s_ctx_ps, g * KD + (k + 1))
                    copy(ctxT[:, k, :], a_bank[k][:, :]).then_inc(s_ctx, 1)

            def sequence(a, g):
                if a is not None:
                    root(s_avar, s_astd, a, amv, astd)
                if g is not None:
                    root(s_var, s_std, g, mv, std)
                if a is not None:
                    copy_T(xaT, a_bank[0:2], s_xaT_ps, s_xaT, a)
                if g is not None:
                    copy_T(xnT, xnT_ps, s_xnT_ps, s_xnT, g)
                if a is not None:
                    copy_qk(a)
                if g is not None:
                    exp_logits(g)
                if a is not None:
                    exp_scores(a)
                if g is not None:
                    shared_silu(g, 0, True)
                if a is not None:
                    copy_probs_T(a)
                if g is not None:
                    shared_silu(g, 1, True)
                if a is not None:
                    copy_context(a)
                if g is not None:
                    shared_silu(g, 2, True)

            act.wait_ge(s_const, CONSTS)
            act.wait_ge(s_load, 16 * LOADS)
            with act.Fori(0, GROUPS) as g:
                ffn_in(g)
            experts(0)
            act.wait_ge(s_bq, 1)
            sequence(0, None)
            with act.Fori(1, GROUPS) as g:
                sequence(g, g + (GROUPS - 1))
            sequence(None, 2 * GROUPS - 1)
            experts(1)
            out_v = out.rearrange("(t p) d -> p t d", p=P)
            with act.Fori(0, GROUPS) as g:
                act.wait_ge(s_added, g * GT + (TILES + GT))
                act.dma_start(out_v[:, bass.ds(g * GT, GT), :], x_res[:, bass.ds(g * GT, GT), :]).then_inc(s_out, 16)
            act.wait_ge(s_out, 16 * GROUPS)

        @block.vector
        def _(dve):
            done = Tally(s_dve)

            def after(n=None, alone=False):
                value = done.at(done.n if n is None else n)
                if alone:
                    wait_alone(dve, s_dve, value)
                else:
                    dve.wait_ge(s_dve, value)

            def x_tile(t):
                return x_res[:, bass.ds(t, 1), :].rearrange("p a d -> p (a d)")

            def norm_stats(t0, s_var_, stats_, mv_):
                for j in range(GT):
                    n = done.add(nc.vector.bn_stats(stats_[:, j, :], x_tile(t0 + j)))
                after(n, alone=True)
                for j in range(GT):
                    i = nc.vector.bn_aggr(mv_[:, j, :], stats_[:, j, :])
                i.then_inc(s_var_, 1)

            def norm(t0, g, dst, mv_, std_, rstd_, s_var_, s_std_, s_done, stored=None):
                dve.wait_ge(s_std_, g + 1)
                done.add(nc.vector.reciprocal(rstd_[:, :], std_[:, :]))
                dve.wait_ge(s_var_, g + 1)
                if stored is not None:
                    dve.wait_ge(s_xn_stored, stored)
                after()
                for j in range(GT):
                    nc.vector.tensor_scalar(dst[:, j, :], x_tile(t0 + j), mv_[:, j, 0:1], rstd_[:, j:j + 1],
                                            ALU.subtract, ALU.mult).then_inc(s_done, 1)

            def over_experts(row):
                return row.rearrange("p (j o) -> p j o", o=1).broadcast_to([P, GT, E])

            def each_key(t):
                return t[:, :, None, :].broadcast_to([P, GT, TOP_K, E])

            def ffn_in(t0, g, first):
                if not first:
                    dve.wait_ge(s_shadd, g * GT)
                after(alone=True)
                norm_stats(t0, s_var, stats, mv)
                norm(t0, g, xn, mv, std, rstd, s_var, s_std, s_xn, None if first else g * 16)
                router_max(g)
                route(g)
                shared_h(g, 0, False)
                slots(g, first)
                shared_h(g, 1, False)
                shared_h(g, 2, False)
                weights(t0)
                shared_add(t0, g)

            def router_max(g):
                wait_alone(dve, s_logits, g + 1)
                nc.vector.tensor_reduce(neg_max[:, :], logits_ps[:, 0:GT * E].rearrange("p (j e) -> p j e", e=E),
                                        axis=AX.X, op=ALU.max, negate=True).then_inc(s_negmax, 1)

            def route(g):
                dve.wait_ge(s_expl, g + 1)
                done.add(nc.vector.reciprocal(rexpsum[:, :], expsum[:, :]))
                after()
                done.add(nc.vector.tensor_tensor(probs[:, :, 0:E], expl[:, :, :], over_experts(rexpsum[:, :]), ALU.mult))
                after(alone=True)
                for j in range(GT):
                    done.add(nc.vector.max(top[:, j, :], probs[:, j, 0:E]))
                after()
                done.add(nc.vector.reduce_sum(topsum[:, :], top[:, :, 0:TOP_K], axis=AX.X))
                n = done.add(nc.vector.tensor_copy(chosen[:, :, 0:TOP_K], top[:, :, 0:TOP_K]))
                after(n, alone=True)
                for j in range(GT):
                    done.add(nc.vector.match_replace(marked[:, j, :], in_to_replace=chosen[:, j, :], in_values=probs[:, j, :], imm_value=-2.0))
                n = done.add(nc.vector.tensor_scalar(topsum[:, :], topsum[:, :], 1e-20, None, ALU.add))
                after(n)
                nc.vector.tensor_scalar(mask[:, :, :], marked[:, :, 0:E], -2.0, None, ALU.is_equal).then_inc(s_mask, 1)
                done.add(nc.vector.reciprocal(rtop[:, :], topsum[:, :]))
                dve.wait_ge(s_mask, g + 1)
                done.add(nc.vector.reduce_sum(mask_sum[:, :], mask[:, :, :].rearrange("p j e -> p e j"), axis=AX.X))
                after()
                done.add(nc.vector.tensor_tensor(wkept[:, :, :], probs[:, :, 0:E], over_experts(rtop[:, :]), ALU.mult))

            def slots(g, first):
                dve.wait_ge(s_pos, g + 1)
                nc.vector.tensor_tensor(before[:, :], before[:, :], mask_sum[:, :], ALU.add).then_inc(s_before, 1)
                pos = pos_ps[:, 0:GT * E].rearrange("p (j e) -> p j e", e=E)
                done.add(nc.vector.scalar_tensor_tensor(out=kept[:, :, :], in0=pos, scalar=float(CAP), in1=mask[:, :, :],
                                                        op0=ALU.is_lt, op1=ALU.mult))
                done.add(nc.vector.tensor_tensor(key[:, :, :], pos, slot_base[:, None, :].broadcast_to([P, GT, E]), ALU.add))
                after()
                n = done.add(nc.vector.tensor_tensor(key[:, :, :], key[:, :, :], kept[:, :, :], ALU.mult))
                done.add(nc.vector.tensor_tensor(wkept[:, :, :], wkept[:, :, :], kept[:, :, :], ALU.mult))
                after(n, alone=True)
                for j in range(GT):
                    done.add(nc.vector.max(top_keys[:, j, :], key[:, j, :]))
                after()
                done.add(nc.vector.tensor_scalar(absent[:, :, :], top_keys[:, :, 0:TOP_K], 0.0, float(NOWHERE), ALU.is_equal, ALU.mult))
                after()
                done.add(nc.vector.tensor_tensor(slot_f[:, :, :], absent[:, :, :], top_keys[:, :, 0:TOP_K], ALU.add))
                after()
                if not first:
                    dve.wait_ge(s_slot_taken, g)
                nc.vector.tensor_scalar(slot_idx[:, :], slot_f[:, :, :].rearrange("p j k -> p (j k)"), -1.0, None,
                                        ALU.add).then_inc(s_slot, 1)

            def weights(t0):
                done.add(nc.vector.tensor_tensor(is_key[:, :, :, :], each_key(key),
                                                 top_keys[:, :, 0:TOP_K].rearrange("p j (k o) -> p j k o", o=1).broadcast_to([P, GT, TOP_K, E]), ALU.is_equal))
                after()
                done.add(nc.vector.tensor_tensor(is_key[:, :, :, :], is_key[:, :, :, :], each_key(wkept), ALU.mult))
                after()
                done.add(nc.vector.reduce_sum(w_row[:, :, :], is_key[:, :, :, :], axis=AX.X))
                after()
                done.add(nc.vector.tensor_scalar(w_tok[:, bass.ds(t0, GT), :], w_row[:, :, :], 0.5, None, ALU.mult))

            def shared_add(t0, g):
                for j in range(GT):
                    dve.wait_ge(s_shout, g * GT + (j + 1))
                    nc.vector.scalar_tensor_tensor(out=x_tile(t0 + j), in0=sho_ps[j % 2][:, 0:D], scalar=0.5, in1=x_tile(t0 + j),
                                                   op0=ALU.mult, op1=ALU.add).then_inc(s_shadd, 1)

            def shared_h(g, c, attending):
                f0, fn = FC[c]
                dve.wait_ge(s_shact, g * len(FC) + (c + 1))
                nc.vector.tensor_tensor(sh_h[0:fn, c, :], sh_act[0:fn, c % 2, :], shgu_ps(c, attending)[1][0:fn, :], ALU.mult).then_inc(s_shh, 1)

            def hidden(o, s, at, b, c):
                dve.wait_ge(o["act"], at["base"] + (s + 1))
                if at["reused"](2):
                    dve.wait_ge(o["hT_ps"], at["base"] + (s - 1))
                nc.vector.tensor_tensor(h[:, s % 2, :], act_g[:, s % 2, :], gu_ps[s % 2][:, F:2 * F], ALU.mult).then_inc(o["h"], 1)

            def copy_hT(o, s, at, b, c):
                dve.wait_ge(o["hT_ps"], at["base"] + (s + 1))
                if at["reused"](2):
                    dve.wait_ge(o["y_ps"], at["base"] + (s - 1))
                nc.vector.tensor_copy(hT[:, s % 2, :, :], hT_ps[s % 2][0:FH, 0:2 * P]).then_inc(o["hT"], 1)

            def over(o):
                def body(q):
                    over_pipeline(dve, o, q, {1: hidden, 2: copy_hT})
                    wait_alone(dve, o["y_ps"], (q + 1) * W_BUFS)
                return body

            def list_over(f):
                dve.wait_ge(s_count_ps, f + 1)
                done.add(nc.vector.tensor_scalar(is_over[:, :], a_bank[0][:, 0:E], float(MAIN), None, ALU.is_gt))
                after()
                done.add(nc.vector.reduce_sum(n_over[:, :], is_over[:, :], axis=AX.X))
                done.add(nc.vector.scalar_tensor_tensor(out=over_key[:, 0, :], in0=is_over[:, :], scalar=float(E),
                                                        in1=expert_id[:, :], op0=ALU.mult, op1=ALU.add))
                after()
                done.add(nc.vector.tensor_copy(n_over_i[:, :], n_over[:, :]))
                for i in range(E // 8):
                    done.add(nc.vector.max(over_sorted[:, i * 8:(i + 1) * 8], over_key[:, i % 2, :]))
                    after()
                    if i < E // 8 - 1:
                        done.add(nc.vector.match_replace(over_key[:, (i + 1) % 2, :], in_to_replace=over_sorted[:, i * 8:(i + 1) * 8],
                                                         in_values=over_key[:, i % 2, :], imm_value=-1.0))
                        after()
                done.add(nc.vector.tensor_copy(over_int[:, :], over_sorted[:, :]))
                after()
                nc.vector.tensor_scalar(over_list[:, :], over_int[:, :], E - 1, None, ALU.bitwise_and).then_inc(s_over_known, 1)

            def experts(f):
                dve.wait_ge(s_table_ps, f + 1)
                nc.vector.tensor_copy(idx[:, :, :], bank[0][:, 0:2 * E * CT]).then_inc(s_idx, 1)
                list_over(f)
                pipeline(dve, f, {1: hidden, 2: copy_hT})
                over_rounds(dve, f, over(s_over[f]))

            def combine(t0, n_back):
                for pair in ((0, 1), (2, 3)):
                    for j in pair:
                        dve.wait_ge(s_back[j], n_back)
                    start = done.n
                    for k in range(TOP_K):
                        for j in pair:
                            if k:
                                after(start + (k - 1) * 2 + j % 2 + 1)
                            i = nc.vector.scalar_tensor_tensor(
                                out=x_tile(t0 + j), in0=back[:, j, k, :],
                                scalar=w_tok[:, bass.ds(t0 + j, 1), k:k + 1].rearrange("p a k -> p (a k)"), in1=x_tile(t0 + j),
                                op0=ALU.mult, op1=ALU.add)
                            if k < TOP_K - 1:
                                done.add(i)
                            else:
                                i.then_inc(s_added, 1)

            def add_v_bias(g):
                for j in range(GT):
                    dve.wait_ge(s_v_ps, g * GT + (j + 1))
                    nc.vector.tensor_tensor(v_sb[:, j, :], a_bank[(2 + j) % 4][:, 0:D], bv_sb[:, :], ALU.add).then_inc(s_v, 1)

            def scores_max(g):
                for j in range(GT):
                    wait_alone(dve, s_score, g * GT + (j + 1))
                    nc.vector.tensor_reduce(neg_row_max[:, j:j + 1], a_bank[(2 + j) % 4][:, :], axis=AX.X, op=ALU.max,
                                            negate=True).then_inc(s_rowmax, 1)

            def add_out(t0, g):
                dve.wait_ge(s_attn, (g + 1) * GT)
                done.add(nc.vector.reciprocal(rattn[:, :], attn_sum[:, :]))
                after()
                for j in range(GT):
                    dve.wait_ge(s_o_ps, g * GT + (j + 1))
                    i = nc.vector.scalar_tensor_tensor(out=x_tile(t0 + j), in0=a_bank[(2 + j) % 4][:, 0:D], scalar=rattn[:, j:j + 1],
                                                       in1=x_tile(t0 + j), op0=ALU.mult, op1=ALU.add)
                i.then_inc(s_projected, 1)

            def sequence(a, g, last=False):
                after(alone=True)
                if a is not None:
                    ta = a * GT
                    if g is not None:
                        dve.wait_ge(s_projected, a)
                    wait_alone(dve, s_added, (a + 1) * GT)
                    norm_stats(ta, s_avar, astats, amv)
                if g is not None:
                    tg = (g - GROUPS) * GT
                    wait_alone(dve, s_shadd, g * GT)
                    if a is None:
                        wait_alone(dve, s_projected, g - (GROUPS - 1))
                    norm_stats(tg, s_var, stats, mv)
                if a is not None:
                    norm(ta, a, xa, amv, astd, arstd, s_avar, s_astd, s_xa)
                if g is not None:
                    norm(tg, g, xn, mv, std, rstd, s_var, s_std, s_xn, g * 16)
                if a is not None:
                    dve.wait_ge(s_xa, (a + 1) * GT)
                    n = done.add(nc.vector.tensor_tensor(x_res[:, bass.ds(ta, GT), :], x_res[:, bass.ds(ta, GT), :],
                                                         bo_sb[:, None, :].broadcast_to([P, GT, D]), ALU.add))
                if g is not None:
                    router_max(g)
                if a is not None:
                    add_v_bias(a)
                if g is not None:
                    route(g)
                if a is not None:
                    scores_max(a)
                if g is not None:
                    slots(g, False)
                    shared_h(g, 0, True)
                    weights(tg)
                    shared_h(g, 1, True)
                    shared_h(g, 2, True)
                if a is not None:
                    after(n)
                    add_out(ta, a)
                if g is not None:
                    shared_add(tg, g)
                if a is not None and not last:
                    combine(ta + GT, a * 16 + 32)

            def start_positions():
                nc.vector.memset(before[:, :], 0.0).then_inc(s_before, 1)

            def repeated(count, start, body, per):
                first_n, base = done.n, done.base
                with dve.Fori(start, start + count) as i:
                    done.base = (i - start) * per if start else i * per
                    body(i)
                    assert done.n - first_n == per, done.n - first_n
                done.base, done.n = base, first_n + per * count

            nc.vector.memset(eps[:, :], EPS).then_inc(s_const, 1)
            nc.vector.memset(blank[:, :], float(NOWHERE)).then_inc(s_zeros, 1)
            nc.vector.memset(zeros[:, :, :], 0.0).then_inc(s_zeros, 1)
            done.add(nc.vector.memset(probs[:, :, E:E + 2], -1.0))
            done.add(nc.vector.memset(chosen[:, :, TOP_K:8], -1.0))
            dve.wait_ge(s_const, CONSTS)
            dve.wait_ge(s_load, 16 * LOADS)
            nc.vector.tensor_scalar(bq_scaled[:, :], bqk_sb[:, 0:KD], float(D) ** -0.5, None, ALU.mult).then_inc(s_bq, 1)
            dve.wait_ge(s_x0, 16)

            start_positions()
            first = done.n
            ffn_in(0, 0, True)
            dve.wait_ge(s_x, 16)
            repeated(GROUPS - 1, 1, lambda g: ffn_in(g * GT, g, False), done.n - first)
            experts(0)

            start_positions()
            dve.wait_ge(s_load_attn, 16 * LOADS_ATTN)
            combine(0, 16)
            sequence(0, None)
            first = done.n
            repeated(GROUPS - 2, 1, lambda a: sequence(a, a + (GROUPS - 1)), SEQUENCE_OPS)
            sequence(GROUPS - 1, 2 * GROUPS - 2, last=True)
            sequence(None, 2 * GROUPS - 1)
            experts(1)
            repeated(GROUPS, 0, lambda g: combine(g * GT, g * 16 + 16 * (GROUPS + 1)), GT * (TOP_K - 1))


SEQUENCE_OPS = 62
_OUT = (B, S, D)


def kernel(L0_attn_hidden_states, L0_attn_w_qkv, L0_attn_b_qkv, L0_attn_w_out, L0_attn_b_out,
           L0_ffn_gate_w, L0_ffn_w_gate, L0_ffn_w_up, L0_ffn_w_down, L0_ffn_sh_gate, L0_ffn_sh_up, L0_ffn_sh_down):
    import concourse.bacc as bacc
    from concourse.bass_utils import run_bass_kernel_spmd

    def chunks(w, p=P):
        w = np.asarray(w).T
        return w.reshape(w.shape[0] // p, p, w.shape[1]).transpose(1, 0, 2)

    w_gu = np.concatenate([np.asarray(L0_ffn_w_gate), np.asarray(L0_ffn_w_up)], axis=1)
    w_gu = w_gu.transpose(0, 2, 1).reshape(E, KD, P, 2 * F).transpose(0, 2, 1, 3).reshape(E * P, KD, 2 * F)
    w_d = np.asarray(L0_ffn_w_down).transpose(0, 2, 1).reshape(E, 2, FH, D).transpose(0, 2, 1, 3).reshape(E * FH, 2, D)
    b = np.asarray(L0_attn_b_qkv)
    arrays = {
        "x": np.asarray(L0_attn_hidden_states).reshape(N, D),
        "wqkv": chunks(L0_attn_w_qkv),
        "woT": chunks(L0_attn_w_out),
        "bqk": b[0:2 * D].reshape(4, P).T,
        "bv": np.broadcast_to(b[2 * D:], (P, D)),
        "bo": np.broadcast_to(np.asarray(L0_attn_b_out), (P, D)),
        "gateT": chunks(L0_ffn_gate_w),
        "w_gu": w_gu,
        "w_d": w_d,
        "sh_g": chunks(L0_ffn_sh_gate),
        "sh_u": chunks(L0_ffn_sh_up),
        "sh_d": np.asarray(L0_ffn_sh_down).T,
    }
    arrays = {name: np.ascontiguousarray(a) for name, a in arrays.items()}
    nc = bacc.Bacc("TRN2", target_bir_lowering=False, num_devices=1)
    aps = {n: nc.dram_tensor(n, a.shape, mybir.dt.from_np(a.dtype), kind="ExternalInput").ap() for n, a in arrays.items()}
    out = nc.dram_tensor("out", (N, D), F32, kind="ExternalOutput").ap()
    build(nc, **aps, out=out)
    got = run_bass_kernel_spmd(nc, [arrays], core_ids=[0])
    return got.results[0]["out"].reshape(_OUT)
```

```python
from contextlib import ExitStack

import numpy as np

import concourse.bass as bass
from concourse import mybir

F32 = mybir.dt.float32
F32R = mybir.dt.float32r
BF16 = mybir.dt.bfloat16
I32 = mybir.dt.int32
U32 = mybir.dt.uint32
ALU = mybir.AluOpType
ACT = mybir.ActivationFunctionType
AX = mybir.AxisListType

P = 128
B, S, D = 4, 512, 256
N = B * S
E, F, FS, TOP_K, CAP_FACTOR = 64, 176, 352, 6, 2
CAP = CAP_FACTOR * ((N * TOP_K + E - 1) // E)
EPS = 1e-5

KD = D // P
TILES = N // P
GROUPS = B
GT = TILES // GROUPS
FH = F // 2
CT = CAP // P
MT = 2
MAIN = MT * P
SLOTS = E * CAP
STEPS = E * MT
SENT = N * TOP_K
NOWHERE = 1 << 20
HALF_TILES = E * CT // 2
FC = [(0, 128), (128, 128), (256, FS - 256)]
FFNS = 2
W_BUFS = 4
W_AHEAD = 2
RAW_GU, RAW_D = KD * 2 * F, 2 * D
X_BUFS = 8
Y_BUFS = 4
ROUND = 16
ROUNDS = STEPS // ROUND
ROUND_E = ROUND // MT
SCATTER_LAG = 8
HALF_WINDOW = ROUND_E * CT // 2
WINDOW_AHEAD = 6
BLANK_ROWS = 12
assert CAP % P == 0 and CT == MT + 1 and STEPS % ROUND == 0 and GT == 4 and KD == 2
assert ROUND == 2 * X_BUFS == 2 * SCATTER_LAG == 4 * Y_BUFS


class Tally:

    def __init__(self, sem):
        self.sem, self.base, self.n = sem, 0, 0

    def add(self, instruction):
        self.n += 1
        instruction.then_inc(self.sem, 1)
        return self.n

    def at(self, n):
        return self.base + n


def build(nc, x, wqkv, woT, bqk, bv, bo, gateT, w_gu, w_d, sh_g, sh_u, sh_d, out):
    table = [nc.dram_tensor(f"table{f}", (SLOTS, 2), F32).ap() for f in range(FFNS)]
    xn_rows = [nc.dram_tensor(f"xn_rows{f}", (N, D), F32).ap() for f in range(FFNS)]
    results = nc.dram_tensor("results", (SENT, D), F32).ap()

    with ExitStack() as ctx:
        def sb(name, shape, dt=F32):
            return ctx.enter_context(nc.sbuf_tensor(name, shape, dt))

        def sem(name):
            return ctx.enter_context(nc.semaphore(name))

        x_res = sb("x_res", [P, TILES, D])
        wqkv_sb = sb("wqkv_sb", [P, KD, 3 * D])
        wo_sb = sb("wo_sb", [P, KD, D])
        bqk_sb = sb("bqk_sb", [P, 4])
        bq_scaled = sb("bq_scaled", [P, KD])
        bv_sb = sb("bv_sb", [P, D])
        bo_sb = sb("bo_sb", [P, D])
        gate_sb = sb("gate_sb", [P, KD, E])
        shg_sb = sb("shg_sb", [P, 2, KD, FS], F32R)
        shu_sb = sb("shu_sb", [P, 2, KD, FS], F32R)
        shd_sb = sb("shd_sb", [P, len(FC), D])
        ident = sb("ident", [P, P])
        earlier = sb("earlier", [P, P], BF16)
        ones = sb("ones", [P, P], BF16)
        slot_base = sb("slot_base", [P, E])
        entry = sb("entry", [P, TILES, TOP_K, 2])
        blank = sb("blank", [P, SLOTS * 2 // P])
        eps = sb("eps", [P, 1])
        stats = sb("stats", [P, GT, 6])
        mv = sb("mv", [P, GT, 2])
        std = sb("std", [P, GT])
        rstd = sb("rstd", [P, GT])
        xn = sb("xn", [P, GT, D])
        xnT = sb("xnT", [P, 2, KD, S], F32R)
        neg_max = sb("neg_max", [P, GT])
        expl = sb("expl", [P, GT, E])
        expsum = sb("expsum", [P, GT])
        rexpsum = sb("rexpsum", [P, GT])
        probs = sb("probs", [P, GT, E + 2])
        top = sb("top", [P, GT, 8])
        chosen = sb("chosen", [P, GT, 8])
        topsum = sb("topsum", [P, GT])
        rtop = sb("rtop", [P, GT])
        marked = sb("marked", [P, GT, E + 2])
        mask = sb("mask", [P, GT, E], BF16)
        mask_sum = sb("mask_sum", [P, E])
        before = sb("before", [P, E], BF16)
        kept = sb("kept", [P, GT, E])
        key = sb("key", [P, GT, E])
        wkept = sb("wkept", [P, GT, E])
        top_keys = sb("top_keys", [P, GT, 8])
        is_key = sb("is_key", [P, GT, TOP_K, E])
        w_row = sb("w_row", [P, GT, TOP_K])
        w_tok = sb("w_tok", [P, TILES, TOP_K])
        absent = sb("absent", [P, GT, TOP_K])
        slot_f = sb("slot_f", [P, GT, TOP_K])
        slot_idx = sb("slot_idx", [P, GT * TOP_K], U32)
        sent_entry = sb("sent_entry", [P, GT, TOP_K, 2])
        sent_idx = sb("sent_idx", [P, GT * TOP_K], U32)
        sh_act = sb("sh_act", [P, 2, S])
        sh_h = sb("sh_h", [P, len(FC), S])
        table_sb = sb("table_sb", [HALF_TILES, 2, 2 * P])
        idx = sb("idx", [P, 2, E * CT + HALF_WINDOW], U32)
        gather_idx = sb("gather_idx", [P, ROUND_E * CT], U32)
        scatter_idx = sb("scatter_idx", [P, ROUND_E * CT], U32)
        expert_id = sb("expert_id", [P, E])
        is_over = sb("is_over", [P, E])
        n_over = sb("n_over", [P, 1])
        n_over_i = sb("n_over_i", [P, 1], I32)
        over_key = sb("over_key", [P, 2, E])
        over_sorted = sb("over_sorted", [P, E])
        over_int = sb("over_int", [P, E], I32)
        over_list = sb("over_list", [P, E], I32)
        wgu_sb = sb("wgu_sb", [P, W_BUFS, 2, KD, 2 * F], F32R)
        wd_sb = sb("wd_sb", [FH, W_BUFS, 2, 2, D], F32R)
        x_sb = sb("x_sb", [P, X_BUFS, D])
        xT = sb("xT", [P, 2, 2, KD, P], F32R)
        act_g = sb("act_g", [P, 2, F])
        h = sb("h", [P, 2, F])
        hT = sb("hT", [FH, 2, 2, 2, P], F32R)
        y_sb = sb("y_sb", [P, Y_BUFS, D])
        over_idx = sb("over_idx", [P, 2, W_BUFS], U32)
        shared = sb("shared", [P, GT * TOP_K * D])
        zeros = shared[:, 0:BLANK_ROWS * D].rearrange("p (n d) -> p n d", d=D)
        raw_gu = [shared[:, b * (RAW_GU + RAW_D):b * (RAW_GU + RAW_D) + RAW_GU].rearrange("p (k f) -> p k f", k=KD)
                  for b in range(W_BUFS)]
        raw_d = [shared[0:FH, b * (RAW_GU + RAW_D) + RAW_GU:(b + 1) * (RAW_GU + RAW_D)].rearrange("p (k d) -> p k d", k=2)
                 for b in range(W_BUFS)]
        back = shared[:, :].rearrange("p (j k d) -> p j k d", j=GT, k=TOP_K)
        astats = sb("astats", [P, GT, 6])
        amv = sb("amv", [P, GT, 2])
        astd = sb("astd", [P, GT])
        arstd = sb("arstd", [P, GT])
        xa = sb("xa", [P, GT, D])
        beside = wgu_sb[:, :, :, :, :].rearrange("p b i k f -> p (b i k f)")
        wqkv_split = beside[:, 0:2 * KD * 3 * D].rearrange("p (i k o) -> p i k o", i=2, k=KD)
        xaT = beside[:, 2 * KD * 3 * D:2 * KD * (3 * D + S)].rearrange("p (i k s) -> p i k s", i=2, k=KD)
        qkT = sb("qkT", [P, 4, S])
        v_sb = sb("v_sb", [P, GT, D])
        neg_row_max = sb("neg_row_max", [P, GT])
        attn = sb("attn", [P, GT, S])
        attn_sum = sb("attn_sum", [P, GT])
        rattn = sb("rattn", [P, GT])
        attnT = sb("attnT", [P, GT, S])
        ctxT = sb("ctxT", [P, KD, S])

        raw = attn[:, :, :].rearrange("p j s -> p (j s)")
        raw_small = [raw[:, c0:c0 + KD * n].rearrange("p (k n) -> p k n", k=KD)
                     for c0, n in ((0, FS), (KD * FS, FS))]
        x_beside = sh_h[:, 0:KD, :]
        x_alone = qkT[:, 0:KD, :]
        def rows_of(memory):
            return memory.rearrange("p (k d) -> p k d", k=TOP_K)
        last_back = [[back[:, j, :, :] for j in range(GT)],
                     [rows_of(t[:, :, :].rearrange("p a b -> p (a b)")[:, 0:TOP_K * D]) for t in (attn, attnT, qkT)] +
                     [rows_of(is_key[:, :, :, :].rearrange("p j k e -> p (j k e)"))]]

        bank = [ctx.enter_context(nc.psum_tensor(f"bank{i}", [P, 512], F32)) for i in range(8)]

        s_x0, s_x = sem("s_x0"), sem("s_x")
        s_load = sem("s_load")
        s_load_attn = sem("s_load_attn")
        s_zeros = sem("s_zeros")
        s_blank = sem("s_blank")
        s_blank_res = sem("s_blank_res")
        s_const = sem("s_const")
        s_bq = sem("s_bq")
        s_pool = sem("s_pool")
        s_dve = sem("s_dve")
        s_var, s_std, s_xn, s_xn_stored = sem("s_var"), sem("s_std"), sem("s_xn"), sem("s_xn_stored")
        s_small_high, s_small = sem("s_small_high"), sem("s_small")
        s_wqkv_high, s_wqkv = sem("s_wqkv_high"), sem("s_wqkv")
        s_xnT_high, s_xnT_low, s_xaT_high = sem("s_xnT_high"), sem("s_xnT_low"), sem("s_xaT_high")
        s_xnT_ps, s_xnT, s_logits, s_negmax = sem("s_xnT_ps"), sem("s_xnT"), sem("s_logits"), sem("s_negmax")
        s_expl, s_mask, s_before, s_pos = sem("s_expl"), sem("s_mask"), sem("s_before"), sem("s_pos")
        s_slot, s_slot_taken, s_sent = sem("s_slot"), sem("s_slot_taken"), sem("s_sent")
        s_entry = sem("s_entry")
        s_shgu, s_shact, s_shh = sem("s_shgu"), sem("s_shact"), sem("s_shh")
        s_shout, s_shadd = sem("s_shout"), sem("s_shadd")
        s_table, s_table_ps, s_idx = sem("s_table"), sem("s_table_ps"), sem("s_idx")
        s_count_ps, s_over_known = sem("s_count_ps"), sem("s_over_known")
        s_wgu = [sem(f"s_wgu{i}") for i in range(W_BUFS)]
        s_wd = [sem(f"s_wd{i}") for i in range(W_BUFS)]
        s_gathered = [sem(f"s_gathered{i}") for i in range(X_BUFS)]
        s_result = [sem(f"s_result{i}") for i in range(Y_BUFS)]
        s_xT_ps, s_xT, s_gu, s_act, s_h = sem("s_xT_ps"), sem("s_xT"), sem("s_gu"), sem("s_act"), sem("s_h")
        s_hT_ps, s_hT, s_y_ps, s_y = sem("s_hT_ps"), sem("s_hT"), sem("s_y_ps"), sem("s_y")
        s_over = [{n: sem(f"s_over_{n}{f}") for n in
                   ("w", "w_high", "w_low", "idx", "x", "xT_ps", "xT_high", "xT", "hT_high", "gu", "act", "h", "hT_ps", "hT", "y_ps", "y", "result")}
                  for f in range(FFNS)]
        s_w_high, s_w_low = sem("s_w_high"), sem("s_w_low")
        s_xT_high, s_hT_high = sem("s_xT_high"), sem("s_hT_high")
        s_windows = sem("s_windows")
        s_experts_done = sem("s_experts_done")
        s_back = [sem(f"s_back{i}") for i in range(GT)]
        s_back_odd = [sem(f"s_back_odd{i}") for i in range(GT)]
        s_weighed, s_pool_added, s_sum = sem("s_weighed"), sem("s_pool_added"), sem("s_sum")
        s_added, s_avar, s_astd, s_xa = sem("s_added"), sem("s_avar"), sem("s_astd"), sem("s_xa")
        s_xaT_ps, s_xaT, s_qk_ps, s_qk = sem("s_xaT_ps"), sem("s_xaT"), sem("s_qk_ps"), sem("s_qk")
        s_v_ps, s_v, s_score, s_rowmax, s_attn = sem("s_v_ps"), sem("s_v"), sem("s_score"), sem("s_rowmax"), sem("s_attn")
        s_attnT_ps, s_attnT, s_ctx_ps, s_ctx = sem("s_attnT_ps"), sem("s_attnT"), sem("s_ctx_ps"), sem("s_ctx")
        s_o_ps, s_projected = sem("s_o_ps"), sem("s_projected")
        s_out = sem("s_out")
        block = ctx.enter_context(nc.Block())

        f_bank, a_bank = bank[0:4], bank[4:8]
        sho_ps = f_bank[2:4]

        def xnT_ps(attending):
            return f_bank[0:2] if attending else a_bank[2:4]

        def logits_ps(attending):
            return f_bank[2] if attending else a_bank[2]

        def shgu_ps(c, attending):
            return f_bank[0:2] if attending or c != 1 else a_bank[0:2]

        xT_ps, gu_ps, hT_ps, y_ps = bank[0:2], bank[2:4], bank[4:6], bank[6:8]

        LOADS = 7
        LOADS_ATTN = 4
        CONSTS = 8
        BLANKS = SENT // P // BLANK_ROWS

        def wait_alone(eng, sem_, value):
            eng.wait_ge(sem_, value)
            eng.nop(nofuse=True)

        main = {"w_high": s_w_high, "w_low": s_w_low, "xT_high": s_xT_high, "hT_high": s_hT_high,
                "xT_ps": s_xT_ps, "xT": s_xT, "gu": s_gu, "act": s_act, "h": s_h, "hT_ps": s_hT_ps,
                "hT": s_hT, "y_ps": s_y_ps, "y": s_y}

        def pipeline(eng, f, stages, before=None):
            def turn(s, at_of):
                for i, stage in stages.items():
                    at = at_of(s - i)
                    if at is not None:
                        t = (s - i) % ROUND
                        stage(main, t, at, t // MT % W_BUFS, t % MT)

            def peeled(t):
                if not 0 <= t < STEPS:
                    return None
                return {"base": f * STEPS + t // ROUND * ROUND, "round": f * ROUNDS + t // ROUND,
                        "tile": t, "over": False, "reused": lambda bufs: f > 0 or t >= bufs}

            for s in range(ROUND):
                if before is not None:
                    before(0, s)
                turn(s, peeled)
            with eng.Fori(1, ROUNDS) as r:
                for s in range(ROUND):
                    if before is not None:
                        before(r, s)
                    def looped(t):
                        back_one = 1 if t < 0 else 0
                        return {"base": r * ROUND + (f * STEPS - ROUND * back_one),
                                "round": r + (f * ROUNDS - back_one),
                                "tile": None, "over": False, "reused": lambda bufs: True}
                    turn(s, looped)
            for s in range(STEPS, STEPS + max(stages)):
                turn(s, peeled)

        def dma_count(at, t, bufs):
            return at["round"] * (16 * (ROUND // bufs)) + 16 * (t // bufs + 1)

        def over_rounds(eng, f, body):
            eng.wait_ge(s_over_known, f + 1)
            n = eng.value_load(n_over_i[0:1, 0:1], min_val=0, max_val=E)
            with eng.If(n > 0):
                body(0)
                with eng.If(n > W_BUFS):
                    with eng.Fori(1, E // W_BUFS) as q:
                        with eng.If(n > q * W_BUFS):
                            body(q)

        def over_pipeline(eng, o, q, stages):
            at = {"base": q * W_BUFS, "round": None, "tile": None, "over": True,
                  "main_results": 16 * (STEPS // Y_BUFS) * (s_over.index(o) + 1)}
            for turn in range(W_BUFS + max(stages)):
                for i, stage in stages.items():
                    s = turn - i
                    if 0 <= s < W_BUFS:
                        stage(o, s, dict(at, reused=lambda bufs, s=s: s >= bufs), s, 0)

        @block.sync
        def _(sp):
            def load_x(g0, g1, s_):
                sp.dma_start(x_res[:, g0 * GT:g1 * GT, :],
                             x[g0 * S:g1 * S, :].rearrange("(t p) d -> p t d", p=P)).then_inc(s_, 16)
            load_x(0, 1, s_x0)
            for dst, src in zip([gate_sb[:, :, :]] + raw_small, (gateT, sh_g, sh_u)):
                sp.dma_start(dst, src).then_inc(s_load, 16)
            for c, (f0, fn) in enumerate(FC):
                sp.dma_start(shd_sb[0:fn, c, :], sh_d[f0:f0 + fn, :]).then_inc(s_load, 16)
            sp.dma_start(bqk_sb[:, :], bqk).then_inc(s_load, 16)
            sp.wait_ge(s_zeros, 1)
            for f in range(FFNS):
                sp.dma_start(table[f].rearrange("(p n) c -> p (n c)", p=P), blank[:, :]).then_inc(s_blank, 16)
            load_x(1, GROUPS, s_x)

            def store_xn(f, g, g_all):
                wait_alone(sp, s_xn, g_all * GT + GT)
                sp.dma_start(xn_rows[f].rearrange("(t p) d -> p t d", p=P)[:, bass.ds(g * GT, GT), :],
                             xn[:, :, :]).then_inc(s_xn_stored, 16)

            def load_expert(b, e, used):
                if used is not None:
                    wait_alone(sp, s_w_low, used)
                sp.dma_start(raw_gu[b], w_gu[bass.ds(e * P, P), :, :]).then_inc(s_wgu[b], 16)
                sp.dma_start(raw_d[b], w_d[bass.ds(e * FH, FH), :, :]).then_inc(s_wd[b], 16)

            def load_first(f):
                if f == 0:
                    sp.wait_ge(s_blank_res, 16 * BLANKS)
                else:
                    sp.wait_ge(s_added, TILES)
                for e in range(W_BUFS):
                    load_expert(e, e, None if f == 0 else f * STEPS + (e - W_BUFS + 1) * MT)

            def load_experts(f):
                for e in range(W_BUFS, ROUND_E):
                    load_expert(e % W_BUFS, e, f * STEPS + (e - W_BUFS + 1) * MT)
                with sp.Fori(1, ROUNDS) as r:
                    for e in range(ROUND_E):
                        load_expert(e % W_BUFS, r * ROUND_E + e, r * ROUND + (f * STEPS + (e - W_BUFS + 1) * MT))

            def over(o):
                def body(q):
                    for b in range(W_BUFS):
                        e = sp.value_load(over_list[0:1, bass.ds(q * W_BUFS + b, 1)], min_val=0, max_val=E - 1)
                        sp.dma_start(raw_gu[b], w_gu[bass.ds(e * P, P), :, :]).then_inc(o["w"], 16)
                        sp.dma_start(raw_d[b], w_d[bass.ds(e * FH, FH), :, :]).then_inc(o["w"], 16)
                    wait_alone(sp, o["w_low"], q * W_BUFS + W_BUFS)
                return body

            def load_table(f):
                sp.wait_ge(s_sent, 16 * GT * TOP_K * GROUPS * (f + 1))
                sp.dma_start(table_sb[:, :, :], table[f].rearrange("(h t s) c -> t h (s c)", h=2, s=P)).then_inc(s_table, 16)

            back_rows = results.rearrange("(t k) c -> t k c", k=TOP_K)

            def load_back(g):
                for j in range(GT):
                    if g is not None:
                        wait_alone(sp, s_added, g * GT + (j + 1 - GT))
                    rows = back_rows[j * P:(j + 1) * P] if g is None else back_rows[bass.ds(g * S + j * P, P), :, :]
                    sp.dma_start(back[:, j, :, :], rows).then_inc(s_back[j], 16)

            def load_last_back(g):
                for j in (0, 1, GT - 1, 2):
                    if g >= 2 and j < GT - 1:
                        sp.wait_ge(s_added, TILES + (g - 2) * (GT - 1) + j + 1)
                    elif g >= 2:
                        sp.wait_ge(s_pool_added, g - 1)
                    sp.dma_start(last_back[g % 2][j], back_rows[g * S + j * P:g * S + (j + 1) * P]).then_inc((s_back, s_back_odd)[g % 2][j], 16)

            sp.wait_ge(s_zeros, 2)
            res = results.rearrange("(g i p n) c -> g i p n c", g=GROUPS, p=P, n=BLANK_ROWS)
            with sp.Fori(0, GROUPS) as g:
                store_xn(0, g, g)
                for i in range(BLANKS // GROUPS):
                    sp.dma_start(res[bass.ds(g, 1), i], zeros).then_inc(s_blank_res, 16)
            for dst, src in ((wqkv_sb, wqkv), (wo_sb, woT)):
                sp.dma_start(dst[:, :, :], src).then_inc(s_load_attn, 16)
            for dst, src in ((bv_sb, bv), (bo_sb, bo)):
                sp.dma_start(dst[:, :], src).then_inc(s_load_attn, 16)
            for f in range(FFNS):
                load_first(f)
                load_table(f)
                load_experts(f)
                sp.wait_ge(s_w_low, STEPS * (f + 1))
                over_rounds(sp, f, over(s_over[f]))
                for i in range(Y_BUFS):
                    sp.wait_ge(s_result[i], 16 * (STEPS // Y_BUFS) * (f + 1))
                sp.wait_ge(s_experts_done, f + 1)
                if f == 0:
                    load_back(None)
                    load_back(1)
                    with sp.Fori(2, GROUPS) as g:
                        load_back(g)
                        store_xn(1, g - 2, g + (GROUPS - 2))
                    for g in range(GROUPS - 2, GROUPS):
                        store_xn(1, g, GROUPS + g)
                else:
                    sp.wait_ge(s_added, TILES)
                    for g in range(GROUPS):
                        load_last_back(g)

        @block.gpsimd
        def _(pool):
            done = Tally(s_pool)
            nc.gpsimd.iota(entry[:, :, :, 0], pattern=[[P, TILES], [0, TOP_K]], base=0,
                           channel_multiplier=1, allow_small_or_imprecise_dtypes=True).then_inc(s_const, 1)
            nc.gpsimd.iota(entry[:, :, :, 1], pattern=[[P * TOP_K, TILES], [1, TOP_K]], base=0,
                           channel_multiplier=TOP_K, allow_small_or_imprecise_dtypes=True).then_inc(s_const, 1)
            done.add(nc.gpsimd.memset(ident[:, :], 1.0))
            n = done.add(nc.gpsimd.memset(earlier[:, :], 1.0))
            nc.gpsimd.memset(ones[:, :], 1.0).then_inc(s_const, 1)
            nc.gpsimd.iota(slot_base[:, :], pattern=[[CAP, E]], base=1, channel_multiplier=0,
                           allow_small_or_imprecise_dtypes=True).then_inc(s_const, 1)
            nc.gpsimd.iota(expert_id[:, :], pattern=[[1, E]], base=0, channel_multiplier=0,
                           allow_small_or_imprecise_dtypes=True).then_inc(s_const, 1)
            pool.wait_ge(s_pool, n)
            nc.gpsimd.affine_select(out=ident[:, :], in_=ident[:, :], compare_op=ALU.is_equal, fill=0.0,
                                    base=0, pattern=[[-1, P]], channel_multiplier=1).then_inc(s_const, 1)
            nc.gpsimd.affine_select(out=earlier[:, :], in_=earlier[:, :], compare_op=ALU.is_gt, fill=0.0,
                                    base=0, pattern=[[1, P]], channel_multiplier=-1).then_inc(s_const, 1)
            nc.gpsimd.memset(x_sb[:, :, :], 0.0).then_inc(s_pool, 1)
            n += 1
            pool.wait_ge(s_pool, n)
            done.n = n
            pool.wait_ge(s_const, CONSTS)

            def send(f, g, g_all, first=False):
                pool.wait_ge(s_slot, g_all + 1)
                if not first:
                    wait_alone(pool, s_sent, g_all * (16 * GT * TOP_K))
                nc.gpsimd.tensor_copy(sent_idx[:, :], slot_idx[:, :]).then_inc(s_slot_taken, 1)
                nc.gpsimd.tensor_copy(sent_entry[:, :, :, :], entry[:, bass.ds(g * GT, GT), :, :]).then_inc(s_entry, 1)
                wait_alone(pool, s_entry, g_all + 1)
                for j in range(GT):
                    for k in range(TOP_K):
                        n_ = j * TOP_K + k
                        nc.gpsimd.indirect_dma_start(
                            out=table[f], out_offset=bass.IndirectOffsetOnAxis(ap=sent_idx[:, n_:n_ + 1], axis=0),
                            in_=sent_entry[:, j, k, :], in_offset=None, bounds_check=SLOTS - 1,
                            oob_is_err=False).then_inc(s_sent, 16)

            def gather_rows(f, dst, idx_, sem_):
                nc.gpsimd.indirect_dma_start(
                    out=dst, out_offset=None, in_=xn_rows[f], in_offset=bass.IndirectOffsetOnAxis(ap=idx_, axis=0),
                    bounds_check=N - 1, oob_is_err=False).then_inc(sem_, 16)

            def scatter_rows(src, idx_, sem_):
                nc.gpsimd.indirect_dma_start(
                    out=results, out_offset=bass.IndirectOffsetOnAxis(ap=idx_, axis=0), in_=src, in_offset=None,
                    bounds_check=SENT - 1, oob_is_err=False).then_inc(sem_, 16)

            def column(s):
                return s // MT * CT + s % MT

            def gather(f):
                def stage(o, s, at, b, c):
                    if at["reused"](X_BUFS):
                        wait_alone(pool, o["xT_ps"], at["base"] + (s + 1 - X_BUFS))
                    i = gather_idx[:, column(s):column(s) + 1] if at["tile"] is None else idx[:, 0, column(at["tile"]):column(at["tile"]) + 1]
                    gather_rows(f, x_sb[:, s % X_BUFS, :], i, s_gathered[s % X_BUFS])
                return stage

            def scatter(o, s, at, b, c):
                wait_alone(pool, o["y"], at["base"] + (s + 1))
                w = (s + SCATTER_LAG) % ROUND
                i = scatter_idx[:, column(w):column(w) + 1] if at["tile"] is None else idx[:, 1, column(at["tile"]):column(at["tile"]) + 1]
                scatter_rows(y_sb[:, s % Y_BUFS, :], i, s_result[s % Y_BUFS])

            def experts(f):
                def indices_there(r, s):
                    if type(r) is not int and s % (ROUND // 2) == 0:
                        wait_alone(pool, s_windows, r * 2 + (f * (2 * ROUNDS - 1) + s // (ROUND // 2) - 1))

                pool.wait_ge(s_idx, f + 1)
                pool.wait_ge(s_xn_stored, 16 * GROUPS * (f + 1))
                pool.wait_ge(s_blank_res, 16 * BLANKS)
                pipeline(pool, f, {0: gather(f), SCATTER_LAG: scatter}, indices_there)
                over_rounds(pool, f, over(f, s_over[f]))
                pool.sem_inc(s_experts_done, 1)

            def over(f, o):
                def body(q):
                    for b in range(W_BUFS):
                        e = pool.value_load(over_list[0:1, bass.ds(q * W_BUFS + b, 1)], min_val=0, max_val=E - 1)
                        nc.gpsimd.tensor_copy(over_idx[:, :, b:b + 1],
                                              idx[:, :, bass.ds(e * CT + MT, 1)]).then_inc(o["idx"], 1)
                    wait_alone(pool, o["idx"], q * W_BUFS + W_BUFS)
                    for b in range(W_BUFS):
                        gather_rows(f, x_sb[:, b, :], over_idx[:, 0, b:b + 1], o["x"])
                    for b in range(W_BUFS):
                        wait_alone(pool, o["y"], q * W_BUFS + (b + 1))
                        scatter_rows(y_sb[:, b, :], over_idx[:, 1, b:b + 1], o["result"])
                    wait_alone(pool, o["x"], (q + 1) * (16 * W_BUFS))
                    wait_alone(pool, o["result"], (q + 1) * (16 * W_BUFS))
                return body

            pool.wait_ge(s_blank, 16 * FFNS)
            send(0, 0, 0, first=True)
            with pool.Fori(1, GROUPS) as g:
                send(0, g, g)
            experts(0)
            with pool.Fori(0, GROUPS) as g:
                send(1, g, g + GROUPS)
            experts(1)
            pool.wait_ge(s_added, TILES)
            own = Tally(s_sum)
            with pool.Fori(0, GROUPS // 2) as pair:
                for i in range(2):
                    g = pair * 2 + i
                    parts = last_back[i][GT - 1]
                    own.base, own.n = g * (TOP_K - 1), 0
                    wait_alone(pool, s_weighed, g + 1)
                    for k in range(1, TOP_K):
                        if own.n:
                            wait_alone(pool, s_sum, own.at(own.n))
                        own.add(nc.gpsimd.tensor_tensor(parts[:, 0, :], parts[:, 0, :], parts[:, k, :], ALU.add))
                    wait_alone(pool, s_sum, own.at(own.n))
                    x_last = x_res[:, bass.ds(g * GT + (GT - 1), 1), :].rearrange("p a d -> p (a d)")
                    nc.gpsimd.tensor_tensor(x_last, x_last, parts[:, 0, :], ALU.add).then_inc(s_pool_added, 1)

        @block.tensor
        def _(pe):
            def mm(out_, lhsT, rhs, first, last):
                return nc.tensor.matmul(out_, lhsT, rhs, start=first, stop=last)

            def products(dst, x_, w, x_cols=slice(None), w_cols=slice(None), parts=((0, 0), (0, 1), (1, 0))):
                for k in range(2):
                    for i, j in parts:
                        m = mm(dst, x_[:, i, k, x_cols], w[:, j, k, w_cols], k == 0 and (i, j) == parts[0],
                               k == 1 and (i, j) == parts[-1])
                return m

            def turn_tiles(dst, src):
                for j in range(GT):
                    for k in range(KD):
                        t = nc.tensor.transpose(dst[k][:, j * P:(j + 1) * P], src[:, j, k * P:(k + 1) * P], ident[:, :])
                return t

            def norms_T(dst, src, s_src, n, s_dst):
                pe.wait_ge(s_src, n)
                turn_tiles(dst, src).then_inc(s_dst, 1)

            def logits(g, attending):
                whole = x_beside if attending else x_alone
                pe.wait_ge(s_xnT, (g + 1) * KD)
                for j in range(GT):
                    for k in range(KD):
                        m = mm(logits_ps(attending)[:, j * E:(j + 1) * E], whole[:, k, j * P:(j + 1) * P],
                               gate_sb[:, k, :], k == 0, k == KD - 1)
                m.then_inc(s_logits, 1)

            def ffn_in(g, first):
                norms_T(xnT_ps(False), xn, s_xn, (g + 1) * GT, s_xnT_ps)
                if not first:
                    shared_down(g - 1)
                logits(g, False)
                shared_up(g, 0, False)
                positions(g, 0, False)
                shared_up(g, 1, False)
                shared_up(g, 2, False)

            def positions(g, f, attending):
                pe.wait_ge(s_mask, g + 1)
                pe.wait_ge(s_before, g + (1 + f))
                for j in range(GT):
                    dst = logits_ps(attending)[:, j * E:(j + 1) * E]
                    mm(dst, earlier[:, :], mask[:, j, :], True, False)
                    for i in range(j):
                        mm(dst, ones[:, :], mask[:, i, :], False, False)
                    m = mm(dst, ones[:, :], before[:, :], False, True)
                m.then_inc(s_pos, 1)

            def shared_up(g, c, attending, x_T=xnT):
                f0, fn = FC[c]
                shg_ps, shu_ps = shgu_ps(c, attending)
                if c == 0:
                    pe.wait_ge(s_xnT_low, (g + 1) * KD)
                if attending and c:
                    pe.wait_ge(s_shh, g * len(FC) + c)
                elif c == 2:
                    pe.wait_ge(s_shh, g * len(FC) + 1)
                products(shg_ps[0:fn, :], shg_sb, x_T, slice(f0, f0 + fn))
                products(shu_ps[0:fn, :], shu_sb, x_T, slice(f0, f0 + fn)).then_inc(s_shgu, 1)

            def shared_down(g):
                pe.wait_ge(s_shh, (g + 1) * len(FC))
                for j in range(GT):
                    if j >= 2:
                        pe.wait_ge(s_shadd, g * GT + (j - 1))
                    for c, (f0, fn) in enumerate(FC):
                        m = mm(sho_ps[j % 2][:, 0:D], sh_h[0:fn, c, j * P:(j + 1) * P], shd_sb[0:fn, c, :],
                               c == 0, c == len(FC) - 1)
                    m.then_inc(s_shout, 1)

            def slots_T(o, s, at, b, c):
                if at["over"]:
                    pe.wait_ge(o["x"], at["base"] * 16 + 16 * W_BUFS)
                else:
                    pe.wait_ge(s_gathered[s % X_BUFS], dma_count(at, s, X_BUFS))
                if at["reused"](2):
                    pe.wait_ge(o["xT"], at["base"] + (s - 1))
                for k in range(KD):
                    t = nc.tensor.transpose(xT_ps[s % 2][:, k * P:(k + 1) * P],
                                            x_sb[:, s % X_BUFS, k * P:(k + 1) * P], ident[:, :])
                t.then_inc(o["xT_ps"], 1)

            def gate_up(o, s, at, b, c):
                if at["over"] or c == 0:
                    pe.wait_ge(o["w_low"], at["base"] + (s + 1))
                pe.wait_ge(o["xT"], at["base"] + (s + 1))
                if at["reused"](2):
                    pe.wait_ge(o["h"], at["base"] + (s - 1))
                products(gu_ps[s % 2][:, 0:2 * F], xT[:, s % 2], wgu_sb[:, b]).then_inc(o["gu"], 1)

            def h_T(o, s, at, b, c):
                pe.wait_ge(o["h"], at["base"] + (s + 1))
                if at["reused"](2):
                    pe.wait_ge(o["hT"], at["base"] + (s - 1))
                for k in range(2):
                    t = nc.tensor.transpose(hT_ps[s % 2][0:FH, k * P:(k + 1) * P],
                                            h[:, s % 2, k * FH:(k + 1) * FH], ident[:, :])
                t.then_inc(o["hT_ps"], 1)

            def down(o, s, at, b, c):
                if c == 0 and not at["over"]:
                    pe.wait_ge(o["w_low"], at["base"] + (s + 2))
                pe.wait_ge(o["hT"], at["base"] + (s + 1))
                if at["reused"](2):
                    pe.wait_ge(o["y"], at["base"] + (s - 1))
                products(y_ps[s % 2][:, 0:D], hT[:, s % 2], wd_sb[:, b]).then_inc(o["y_ps"], 1)

            def over(o):
                def body(q):
                    over_pipeline(pe, o, q, {1: slots_T, 2: gate_up, 3: h_T, 4: down})
                    wait_alone(pe, o["y"], (q + 1) * W_BUFS)
                return body

            def count_tokens(f):
                pe.wait_ge(s_before, GROUPS * (f + 1) + f + 1)
                mm(a_bank[3][:, 0:E], ones[:, :], before[:, :], True, True).then_inc(s_count_ps, 1)

            def experts(f):
                pe.wait_ge(s_shadd, TILES * (f + 1))
                pe.wait_ge(s_table, 16 * (f + 1))
                for w in range(2):
                    for half in range(2):
                        at = (w * 2 + half) * HALF_TILES
                        t = nc.tensor.transpose(bank[0][:, at:at + HALF_TILES],
                                                table_sb[:, half, w:2 * P:2], ident[0:HALF_TILES, 0:HALF_TILES])
                t.then_inc(s_table_ps, 1)
                pe.wait_ge(s_idx, f + 1)
                pe.wait_ge(s_over_known, f + 1)
                pipeline(pe, f, {W_AHEAD: slots_T, W_AHEAD + 1: gate_up, W_AHEAD + 2: h_T, W_AHEAD + 3: down})
                pe.wait_ge(s_y, STEPS * (f + 1))
                over_rounds(pe, f, over(s_over[f]))

            def qk(g):
                pe.wait_ge(s_xaT, (g + 1) * KD)
                for m_ in range(4):
                    products(a_bank[(2 + m_) % 4][:, :], wqkv_split, xaT, slice(m_ * P, (m_ + 1) * P)).then_inc(s_qk_ps, 1)

            def v(g):
                for j in range(GT):
                    pe.wait_ge(s_qk, g * 4 + (j + 1))
                    products(a_bank[(2 + j) % 4][:, 0:D], xaT, wqkv_split, slice(j * P, (j + 1) * P),
                             slice(2 * D, 3 * D)).then_inc(s_v_ps, 1)

            def scores(g):
                for j in range(GT):
                    pe.wait_ge(s_v, g * GT + (j + 1))
                    for k in range(KD):
                        m = mm(a_bank[(2 + j) % 4][:, :], qkT[:, k, j * P:(j + 1) * P], qkT[:, KD + k, :], k == 0, k == KD - 1)
                    m.then_inc(s_score, 1)

            def probs_T(g):
                pe.wait_ge(s_attn, (g + 1) * GT)
                for j in range(GT):
                    for c in range(GT):
                        t = nc.tensor.transpose(a_bank[c][:, j * P:(j + 1) * P], attn[:, j, c * P:(c + 1) * P],
                                                ident[:, :])
                t.then_inc(s_attnT_ps, 1)

            def context(g):
                for m_ in range(KD):
                    for c in range(GT):
                        if m_ == 0:
                            pe.wait_ge(s_attnT, g * GT + (c + 1))
                        m = mm(a_bank[m_][:, :], v_sb[:, c, m_ * P:(m_ + 1) * P], attnT[:, c, :], c == 0, c == GT - 1)
                    m.then_inc(s_ctx_ps, 1)

            def project(g):
                pe.wait_ge(s_ctx, (g + 1) * KD)
                for j in range(GT):
                    for k in range(KD):
                        m = mm(a_bank[(2 + j) % 4][:, 0:D], ctxT[:, k, j * P:(j + 1) * P], wo_sb[:, k, :], k == 0, k == KD - 1)
                    m.then_inc(s_o_ps, 1)

            def sequence(a, g, last=False):
                if a is not None:
                    if g is not None:
                        pe.wait_ge(s_projected, a)
                    norms_T(a_bank[0:2], xa, s_xa, (a + 1) * GT, s_xaT_ps)
                    qk(a)
                if g is not None:
                    norms_T(xnT_ps(True), xn, s_xn, (g + 1) * GT, s_xnT_ps)
                if a is not None:
                    v(a)
                if g is not None:
                    logits(g, True)
                if a is not None:
                    scores(a)
                sharing = g is not None and not last
                if sharing:
                    shared_up(g, 0, True)
                if g is not None:
                    positions(g, 1, True)
                if a is not None:
                    probs_T(a)
                if sharing:
                    shared_up(g, 1, True)
                if a is not None:
                    context(a)
                if sharing:
                    shared_up(g, 2, True)
                if a is not None:
                    project(a)
                if sharing:
                    shared_down(g)

            def last_group(g):
                shared_up(g - 1, 0, False)
                norms_T(xnT_ps(False), xn, s_xn, (g + 1) * GT, s_xnT_ps)
                logits(g, False)
                shared_up(g - 1, 1, False)
                positions(g, 1, False)
                shared_up(g - 1, 2, False)
                shared_down(g - 1)
                count_tokens(1)
                for c in range(len(FC)):
                    shared_up(g, c, False, xaT)
                shared_down(g)

            pe.wait_ge(s_const, CONSTS)
            pe.wait_ge(s_load, 16 * LOADS)
            pe.wait_ge(s_small, 2)
            ffn_in(0, True)
            with pe.Fori(1, GROUPS) as g:
                ffn_in(g, False)
            count_tokens(0)
            shared_down(GROUPS - 1)
            experts(0)
            pe.wait_ge(s_load_attn, 16 * LOADS_ATTN)
            pe.wait_ge(s_wqkv, 1)
            sequence(0, None)
            with pe.Fori(1, GROUPS - 1) as g:
                sequence(g, g + (GROUPS - 1))
            sequence(GROUPS - 1, 2 * GROUPS - 2, last=True)
            last_group(2 * GROUPS - 1)
            experts(1)

        @block.scalar
        def _(act):
            def copy(out_, in_):
                return nc.scalar.activation(out_, in_, ACT.Copy)

            def root(s_var_, s_std_, g, mv_, std_):
                act.wait_ge(s_var_, g + 1)
                nc.scalar.activation(std_[:, :], mv_[:, :, 1], ACT.Sqrt, bias=eps[:, 0:1]).then_inc(s_std_, 1)

            def copy_T(dst, src, s_src, s_dst, g):
                act.wait_ge(s_src, g + 1)
                for k in range(KD):
                    copy(dst[:, k, :], src[k][:, :]).then_inc(s_dst, 1)

            def routed_T(dst, g, attending):
                whole = x_beside if attending else x_alone
                copy_T(whole, xnT_ps(attending), s_xnT_ps, s_xnT, g)
                act.wait_ge(s_xnT, (g + 1) * KD)
                copy(dst[:, 0, :, :], whole).then_inc(s_xnT_high, 1)

            def exp_logits(g, attending):
                act.wait_ge(s_negmax, g + 1)
                for j in range(GT):
                    e = nc.scalar.activation(expl[:, j, :], logits_ps(attending)[:, j * E:(j + 1) * E], ACT.Exp,
                                             bias=neg_max[:, j:j + 1], accum_out=expsum[:, j:j + 1])
                e.then_inc(s_expl, 1)

            def shared_silu(g, c, attending):
                fn = FC[c][1]
                act.wait_ge(s_shgu, g * len(FC) + (c + 1))
                if c == 2:
                    act.wait_ge(s_shh, g * len(FC) + 1)
                nc.scalar.activation(sh_act[0:fn, c % 2, :], shgu_ps(c, attending)[0][0:fn, :], ACT.Silu).then_inc(s_shact, 1)

            def ffn_in(g, last=False):
                routed_T(xnT, g, False)
                exp_logits(g, False)
                shared_silu(g, 0, False)
                shared_silu(g, 1, False)
                if not last:
                    root(s_var, s_std, g + 1, mv, std)
                shared_silu(g, 2, False)

            def copy_slots_T(o, s, at, b, c):
                act.wait_ge(o["xT_ps"], at["base"] + (s + 1))
                if at["reused"](2):
                    act.wait_ge(o["gu"], at["base"] + (s - 1))
                copy(xT[:, s % 2, 0, :, :], xT_ps[s % 2][:, 0:KD * P]).then_inc(o["xT_high"], 1)

            def weights_high(o, s, at, b, c):
                if at["over"] or c == 0:
                    if at["over"]:
                        act.wait_ge(o["w"], at["base"] * 32 + 32 * W_BUFS)
                    else:
                        act.wait_ge(s_wgu[b], dma_count(at, s, W_BUFS * MT))
                    if at["reused"](W_BUFS * MT):
                        act.wait_ge(o["gu"], at["base"] + (s + MT - W_BUFS * MT))
                    i = copy(wgu_sb[:, b, 0, :, :], raw_gu[b])
                    if not at["over"]:
                        i.then_inc(o["w_high"], 1)
                if at["over"] or c == 1:
                    if not at["over"]:
                        act.wait_ge(s_wd[b], dma_count(at, s, W_BUFS * MT))
                    if at["reused"](W_BUFS * MT):
                        act.wait_ge(o["y_ps"], at["base"] + (s + 1 - W_BUFS * MT))
                    copy(wd_sb[:, b, 0, :, :], raw_d[b]).then_inc(o["w_high"], 1)

            def copy_hT(o, s, at, b, c):
                act.wait_ge(o["hT_ps"], at["base"] + (s + 1))
                if at["reused"](2):
                    act.wait_ge(o["y_ps"], at["base"] + (s - 1))
                copy(hT[:, s % 2, 0, :, :], hT_ps[s % 2][0:FH, 0:2 * P]).then_inc(o["hT_high"], 1)

            def silu(o, s, at, b, c):
                act.wait_ge(o["gu"], at["base"] + (s + 1))
                if at["reused"](2):
                    act.wait_ge(o["h"], at["base"] + (s - 1))
                nc.scalar.activation(act_g[:, s % 2, :], gu_ps[s % 2][:, 0:F], ACT.Silu).then_inc(o["act"], 1)

            def copy_y(o, s, at, b, c):
                act.wait_ge(o["y_ps"], at["base"] + (s + 1))
                if at["over"]:
                    act.wait_ge(s_result[s], at["main_results"])
                elif at["reused"](Y_BUFS):
                    act.wait_ge(s_result[s % Y_BUFS], dma_count(at, s - Y_BUFS, Y_BUFS))
                copy(y_sb[:, s % Y_BUFS, :], y_ps[s % 2][:, 0:D]).then_inc(o["y"], 1)

            def over(o):
                def body(q):
                    over_pipeline(act, o, q, {0: weights_high, 1: copy_slots_T, 2: silu, 3: copy_hT, 4: copy_y})
                    wait_alone(act, o["result"], (q + 1) * (16 * W_BUFS))
                return body

            def experts(f):
                pipeline(act, f, {W_AHEAD: copy_slots_T, 0: weights_high, W_AHEAD + 1: silu, W_AHEAD + 2: copy_hT,
                                  W_AHEAD + 3: copy_y})
                over_rounds(act, f, over(s_over[f]))

            def copy_qk(g):
                for m_ in range(4):
                    act.wait_ge(s_qk_ps, g * 4 + (m_ + 1))
                    nc.scalar.activation(qkT[:, m_, :], a_bank[(2 + m_) % 4][:, :], ACT.Identity,
                                         bias=bq_scaled[:, m_:m_ + 1] if m_ < KD else bqk_sb[:, m_:m_ + 1],
                                         scale=float(D) ** -0.5 if m_ < KD else 1.0).then_inc(s_qk, 1)

            def exp_scores(g):
                for j in range(GT):
                    act.wait_ge(s_rowmax, g * GT + (j + 1))
                    nc.scalar.activation(attn[:, j, :], a_bank[(2 + j) % 4][:, :], ACT.Exp, bias=neg_row_max[:, j:j + 1],
                                         accum_out=attn_sum[:, j:j + 1]).then_inc(s_attn, 1)

            def copy_probs_T(g):
                act.wait_ge(s_attnT_ps, g + 1)
                for c in range(GT):
                    copy(attnT[:, c, :], a_bank[c][:, :]).then_inc(s_attnT, 1)

            def copy_context(g):
                for k in range(KD):
                    act.wait_ge(s_ctx_ps, g * KD + (k + 1))
                    copy(ctxT[:, k, :], a_bank[k][:, :]).then_inc(s_ctx, 1)

            def sequence(a, g, last=False):
                if a is not None:
                    copy_T(xaT[:, 0], a_bank[0:2], s_xaT_ps, s_xaT_high, a)
                if g is not None:
                    root(s_var, s_std, g, mv, std)
                if a is not None:
                    copy_qk(a)
                if g is not None:
                    routed_T(xnT, g, True)
                    exp_logits(g, True)
                if a is not None:
                    exp_scores(a)
                    if not last:
                        root(s_avar, s_astd, a + 1, amv, astd)
                sharing = g is not None and not last
                if sharing:
                    shared_silu(g, 0, True)
                if a is not None:
                    copy_probs_T(a)
                if sharing:
                    shared_silu(g, 1, True)
                if a is not None:
                    copy_context(a)
                if sharing:
                    shared_silu(g, 2, True)

            def last_group(g):
                root(s_var, s_std, g, mv, std)
                shared_silu(g - 1, 0, False)
                routed_T(xaT, g, False)
                exp_logits(g, False)
                shared_silu(g - 1, 1, False)
                shared_silu(g - 1, 2, False)
                for c in range(len(FC)):
                    shared_silu(g, c, False)

            act.wait_ge(s_const, CONSTS)
            act.wait_ge(s_load, 16 * LOADS)
            for dst, src in zip((shg_sb, shu_sb), raw_small):
                copy(dst[:, 0, :, :], src).then_inc(s_small_high, 1)
            root(s_var, s_std, 0, mv, std)
            with act.Fori(0, GROUPS - 1) as g:
                ffn_in(g)
            ffn_in(GROUPS - 1, last=True)
            experts(0)
            act.wait_ge(s_bq, 1)
            act.wait_ge(s_load_attn, 16 * LOADS_ATTN)
            copy(wqkv_split[:, 0, :, :], wqkv_sb[:, :, :]).then_inc(s_wqkv_high, 1)
            root(s_avar, s_astd, 0, amv, astd)
            sequence(0, None)
            with act.Fori(1, GROUPS - 1) as g:
                sequence(g, g + (GROUPS - 1))
            sequence(GROUPS - 1, 2 * GROUPS - 2, last=True)
            last_group(2 * GROUPS - 1)
            experts(1)
            out_v = out.rearrange("(t p) d -> p t d", p=P)
            act.wait_ge(s_added, TILES)
            with act.Fori(0, GROUPS // 2) as pair:
                for i in range(2):
                    act.wait_ge((s_back, s_back_odd)[i][GT - 1], pair * 16 + (16, 0)[i] * GROUPS + 16)
                    for k in range(TOP_K):
                        part = last_back[i][GT - 1][:, k, :]
                        tile = bass.ds(pair * (2 * GT) + (i * GT + GT - 1), 1)
                        weighed = nc.scalar.activation(part, part, ACT.Copy,
                                                       scale=w_tok[:, tile, k:k + 1].rearrange("p a k -> p (a k)"))
                    weighed.then_inc(s_weighed, 1)
                for i in range(2):
                    g = pair * 2 + i
                    act.wait_ge(s_added, g * (GT - 1) + (TILES + GT - 1))
                    act.wait_ge(s_pool_added, g + 1)
                    act.dma_start(out_v[:, bass.ds(g * GT, GT), :], x_res[:, bass.ds(g * GT, GT), :]).then_inc(s_out, 16)
            act.wait_ge(s_out, 16 * GROUPS)

        @block.vector
        def _(dve):
            done = Tally(s_dve)

            def after(n=None, alone=False):
                value = done.at(done.n if n is None else n)
                if alone:
                    wait_alone(dve, s_dve, value)
                else:
                    dve.wait_ge(s_dve, value)

            def x_tile(t):
                return x_res[:, bass.ds(t, 1), :].rearrange("p a d -> p (a d)")

            def low(out_, whole, high):
                return nc.vector.tensor_tensor(out_, whole, high, ALU.subtract)

            def attention_low(a):
                for k in range(KD):
                    dve.wait_ge(s_xaT_high, a * KD + (k + 1))
                    low(xaT[:, 1, k, :], a_bank[k][:, :], xaT[:, 0, k, :]).then_inc(s_xaT, 1)

            def routed_low(dst, g, attending):
                dve.wait_ge(s_xnT_high, g + 1)
                low(dst[:, 1, :, :], x_beside if attending else x_alone, dst[:, 0, :, :]).then_inc(s_xnT_low, KD)

            def norm_stats(t0, s_var_, stats_, mv_):
                for j in range(GT):
                    n = done.add(nc.vector.bn_stats(stats_[:, j, :], x_tile(t0 + j)))
                after(n, alone=True)
                for j in range(GT):
                    i = nc.vector.bn_aggr(mv_[:, j, :], stats_[:, j, :])
                i.then_inc(s_var_, 1)

            def norm(t0, g, dst, mv_, std_, rstd_, s_var_, s_std_, s_done, stored=None):
                dve.wait_ge(s_std_, g + 1)
                done.add(nc.vector.reciprocal(rstd_[:, :], std_[:, :]))
                dve.wait_ge(s_var_, g + 1)
                if stored is not None:
                    dve.wait_ge(s_xn_stored, stored)
                after()
                for j in range(GT):
                    nc.vector.tensor_scalar(dst[:, j, :], x_tile(t0 + j), mv_[:, j, 0:1], rstd_[:, j:j + 1],
                                            ALU.subtract, ALU.mult).then_inc(s_done, 1)

            def over_experts(row):
                return row.rearrange("p (j o) -> p j o", o=1).broadcast_to([P, GT, E])

            def each_key(t):
                return t[:, :, None, :].broadcast_to([P, GT, TOP_K, E])

            def ffn_in(t0, g, first=False, last=False):
                if not first:
                    shared_add(t0 - GT, g - 1)
                    weights(t0 - GT)
                router_max(g, False)
                routed_low(xnT, g, False)
                route(g)
                slots(g, first, False)
                shared_h(g, 0, False)
                if not last:
                    after(alone=True)
                    norm_stats(t0 + GT, s_var, stats, mv)
                shared_h(g, 1, False)
                if not last:
                    norm(t0 + GT, g + 1, xn, mv, std, rstd, s_var, s_std, s_xn, (g + 1) * 16)
                shared_h(g, 2, False)

            def router_max(g, attending):
                wait_alone(dve, s_logits, g + 1)
                nc.vector.tensor_reduce(neg_max[:, :], logits_ps(attending)[:, 0:GT * E].rearrange("p (j e) -> p j e", e=E),
                                        axis=AX.X, op=ALU.max, negate=True).then_inc(s_negmax, 1)

            def route(g):
                dve.wait_ge(s_expl, g + 1)
                done.add(nc.vector.reciprocal(rexpsum[:, :], expsum[:, :]))
                after()
                done.add(nc.vector.tensor_tensor(probs[:, :, 0:E], expl[:, :, :], over_experts(rexpsum[:, :]), ALU.mult))
                after(alone=True)
                for j in range(GT):
                    done.add(nc.vector.max(top[:, j, :], probs[:, j, 0:E]))
                after()
                done.add(nc.vector.reduce_sum(topsum[:, :], top[:, :, 0:TOP_K], axis=AX.X))
                n = done.add(nc.vector.tensor_copy(chosen[:, :, 0:TOP_K], top[:, :, 0:TOP_K]))
                after(n, alone=True)
                for j in range(GT):
                    done.add(nc.vector.match_replace(marked[:, j, :], in_to_replace=chosen[:, j, :], in_values=probs[:, j, :], imm_value=-2.0))
                n = done.add(nc.vector.tensor_scalar(topsum[:, :], topsum[:, :], 1e-20, None, ALU.add))
                after(n)
                nc.vector.tensor_scalar(mask[:, :, :], marked[:, :, 0:E], -2.0, None, ALU.is_equal).then_inc(s_mask, 1)
                done.add(nc.vector.reciprocal(rtop[:, :], topsum[:, :]))
                dve.wait_ge(s_mask, g + 1)
                done.add(nc.vector.reduce_sum(mask_sum[:, :], mask[:, :, :].rearrange("p j e -> p e j"), axis=AX.X))
                after()
                done.add(nc.vector.tensor_tensor(wkept[:, :, :], probs[:, :, 0:E], over_experts(rtop[:, :]), ALU.mult))

            def slots(g, first, attending):
                dve.wait_ge(s_pos, g + 1)
                nc.vector.tensor_tensor(before[:, :], before[:, :], mask_sum[:, :], ALU.add).then_inc(s_before, 1)
                pos = logits_ps(attending)[:, 0:GT * E].rearrange("p (j e) -> p j e", e=E)
                done.add(nc.vector.scalar_tensor_tensor(out=kept[:, :, :], in0=pos, scalar=float(CAP), in1=mask[:, :, :],
                                                        op0=ALU.is_lt, op1=ALU.mult))
                done.add(nc.vector.tensor_tensor(key[:, :, :], pos, slot_base[:, None, :].broadcast_to([P, GT, E]), ALU.add))
                after()
                n = done.add(nc.vector.tensor_tensor(key[:, :, :], key[:, :, :], kept[:, :, :], ALU.mult))
                done.add(nc.vector.tensor_tensor(wkept[:, :, :], wkept[:, :, :], kept[:, :, :], ALU.mult))
                after(n, alone=True)
                for j in range(GT):
                    done.add(nc.vector.max(top_keys[:, j, :], key[:, j, :]))
                after()
                done.add(nc.vector.tensor_scalar(absent[:, :, :], top_keys[:, :, 0:TOP_K], 0.0, float(NOWHERE), ALU.is_equal, ALU.mult))
                after()
                done.add(nc.vector.tensor_tensor(slot_f[:, :, :], absent[:, :, :], top_keys[:, :, 0:TOP_K], ALU.add))
                after()
                if not first:
                    dve.wait_ge(s_slot_taken, g)
                nc.vector.tensor_scalar(slot_idx[:, :], slot_f[:, :, :].rearrange("p j k -> p (j k)"), -1.0, None,
                                        ALU.add).then_inc(s_slot, 1)

            def weights(t0):
                done.add(nc.vector.tensor_tensor(is_key[:, :, :, :], each_key(key),
                                                 top_keys[:, :, 0:TOP_K].rearrange("p j (k o) -> p j k o", o=1).broadcast_to([P, GT, TOP_K, E]), ALU.is_equal))
                after()
                done.add(nc.vector.tensor_tensor(is_key[:, :, :, :], is_key[:, :, :, :], each_key(wkept), ALU.mult))
                after()
                done.add(nc.vector.reduce_sum(w_row[:, :, :], is_key[:, :, :, :], axis=AX.X))
                after()
                done.add(nc.vector.tensor_scalar(w_tok[:, bass.ds(t0, GT), :], w_row[:, :, :], 0.5, None, ALU.mult))

            def shared_add(t0, g):
                for j in range(GT):
                    dve.wait_ge(s_shout, g * GT + (j + 1))
                    nc.vector.scalar_tensor_tensor(out=x_tile(t0 + j), in0=sho_ps[j % 2][:, 0:D], scalar=0.5, in1=x_tile(t0 + j),
                                                   op0=ALU.mult, op1=ALU.add).then_inc(s_shadd, 1)

            def shared_h(g, c, attending):
                f0, fn = FC[c]
                dve.wait_ge(s_shact, g * len(FC) + (c + 1))
                nc.vector.tensor_tensor(sh_h[0:fn, c, :], sh_act[0:fn, c % 2, :], shgu_ps(c, attending)[1][0:fn, :], ALU.mult).then_inc(s_shh, 1)

            def hidden(o, s, at, b, c):
                dve.wait_ge(o["act"], at["base"] + (s + 1))
                if at["reused"](2):
                    dve.wait_ge(o["hT_ps"], at["base"] + (s - 1))
                nc.vector.tensor_tensor(h[:, s % 2, :], act_g[:, s % 2, :], gu_ps[s % 2][:, F:2 * F], ALU.mult).then_inc(o["h"], 1)

            def slots_low(o, s, at, b, c):
                dve.wait_ge(o["xT_high"], at["base"] + (s + 1))
                if at["reused"](2):
                    dve.wait_ge(o["gu"], at["base"] + (s - 1))
                low(xT[:, s % 2, 1, :, :], xT_ps[s % 2][:, 0:KD * P].rearrange("p (k t) -> p k t", k=KD),
                    xT[:, s % 2, 0, :, :]).then_inc(o["xT"], 1)

            def hT_low(o, s, at, b, c):
                dve.wait_ge(o["hT_high"], at["base"] + (s + 1))
                if at["reused"](2):
                    dve.wait_ge(o["y_ps"], at["base"] + (s - 1))
                low(hT[:, s % 2, 1, :, :], hT_ps[s % 2][0:FH, 0:2 * P].rearrange("p (k t) -> p k t", k=2),
                    hT[:, s % 2, 0, :, :]).then_inc(o["hT"], 1)

            def weights_low(o, s, at, b, c):
                dve.wait_ge(o["w_high"], at["base"] + (s + 1))
                if at["over"] or c == 0:
                    i = low(wgu_sb[:, b, 1, :, :], raw_gu[b], wgu_sb[:, b, 0, :, :])
                    if not at["over"]:
                        i.then_inc(o["w_low"], 1)
                if at["over"] or c == 1:
                    low(wd_sb[:, b, 1, :, :], raw_d[b], wd_sb[:, b, 0, :, :]).then_inc(o["w_low"], 1)

            def over(o):
                def body(q):
                    over_pipeline(dve, o, q, {0: weights_low, 1: slots_low, 2: hidden, 3: hT_low})
                    wait_alone(dve, o["y_ps"], (q + 1) * W_BUFS)
                return body

            def list_over(f):
                dve.wait_ge(s_count_ps, f + 1)
                done.add(nc.vector.tensor_scalar(is_over[:, :], a_bank[3][:, 0:E], float(MAIN), None, ALU.is_gt))
                after()
                done.add(nc.vector.reduce_sum(n_over[:, :], is_over[:, :], axis=AX.X))
                done.add(nc.vector.scalar_tensor_tensor(out=over_key[:, 0, :], in0=is_over[:, :], scalar=float(E),
                                                        in1=expert_id[:, :], op0=ALU.mult, op1=ALU.add))
                after()
                done.add(nc.vector.tensor_copy(n_over_i[:, :], n_over[:, :]))
                for i in range(E // 8):
                    done.add(nc.vector.max(over_sorted[:, i * 8:(i + 1) * 8], over_key[:, i % 2, :]))
                    after()
                    if i < E // 8 - 1:
                        done.add(nc.vector.match_replace(over_key[:, (i + 1) % 2, :], in_to_replace=over_sorted[:, i * 8:(i + 1) * 8],
                                                         in_values=over_key[:, i % 2, :], imm_value=-1.0))
                        after()
                done.add(nc.vector.tensor_copy(over_int[:, :], over_sorted[:, :]))
                after()
                nc.vector.tensor_scalar(over_list[:, :], over_int[:, :], E - 1, None, ALU.bitwise_and).then_inc(s_over_known, 1)

            def experts(f):
                dve.wait_ge(s_table_ps, f + 1)
                nc.vector.tensor_copy(idx[:, :, 0:E * CT], bank[0][:, 0:2 * E * CT]).then_inc(s_idx, 1)
                lag = SCATTER_LAG // MT * CT

                def put_indices(r, s):
                    if (s + WINDOW_AHEAD) % (ROUND // 2) or (type(r) is int and s + WINDOW_AHEAD < ROUND):
                        return
                    half, later = (s + WINDOW_AHEAD) % ROUND // (ROUND // 2), (s + WINDOW_AHEAD) // ROUND
                    for s_ in s_gathered:
                        dve.wait_ge(s_, r * 32 + (2 * later + half - 1 + f * 2 * ROUNDS) * 16)
                    if f or type(r) is not int:
                        for s_ in s_result:
                            dve.wait_ge(s_, r * 64 + ((later - 1) * 64 + half * 32 + f * STEPS * 16 // Y_BUFS))
                    dve.nop(nofuse=True)
                    first = r * (2 * HALF_WINDOW) + (later * 2 + half) * HALF_WINDOW
                    cols = slice(half * HALF_WINDOW, (half + 1) * HALF_WINDOW)
                    nc.vector.tensor_copy(gather_idx[:, cols], idx[:, 0, bass.ds(first, HALF_WINDOW)])
                    nc.vector.tensor_copy(scatter_idx[:, cols], idx[:, 1, bass.ds(first - lag, HALF_WINDOW)]).then_inc(s_windows, 1)

                dve.wait_ge(s_idx, f + 1)
                pipeline(dve, f, {W_AHEAD: slots_low, 0: weights_low, W_AHEAD + 1: hidden, W_AHEAD + 2: hT_low}, put_indices)
                over_rounds(dve, f, over(s_over[f]))

            PAIRS = ((0, 1), (2, 3))

            def combine(t0, n_back, pairs=PAIRS, bufs=last_back[0], s_back=s_back):
                for pair in pairs:
                    for j in pair:
                        dve.wait_ge(s_back[j], n_back)
                    start = done.n
                    for k in range(TOP_K):
                        for j in pair:
                            if k:
                                after(start + (k - 1) * len(pair) + j % 2 + 1)
                            i = nc.vector.scalar_tensor_tensor(
                                out=x_tile(t0 + j), in0=bufs[j][:, k, :],
                                scalar=w_tok[:, bass.ds(t0 + j, 1), k:k + 1].rearrange("p a k -> p (a k)"), in1=x_tile(t0 + j),
                                op0=ALU.mult, op1=ALU.add)
                            if k < TOP_K - 1:
                                done.add(i)
                            else:
                                i.then_inc(s_added, 1)

            def add_v_bias(g):
                for j in range(GT):
                    dve.wait_ge(s_v_ps, g * GT + (j + 1))
                    nc.vector.tensor_tensor(v_sb[:, j, :], a_bank[(2 + j) % 4][:, 0:D], bv_sb[:, :], ALU.add).then_inc(s_v, 1)

            def scores_max(g):
                for j in range(GT):
                    wait_alone(dve, s_score, g * GT + (j + 1))
                    nc.vector.tensor_reduce(neg_row_max[:, j:j + 1], a_bank[(2 + j) % 4][:, :], axis=AX.X, op=ALU.max,
                                            negate=True).then_inc(s_rowmax, 1)

            def add_out(t0, g):
                dve.wait_ge(s_attn, (g + 1) * GT)
                done.add(nc.vector.reciprocal(rattn[:, :], attn_sum[:, :]))
                after()
                for j in range(GT):
                    dve.wait_ge(s_o_ps, g * GT + (j + 1))
                    i = nc.vector.scalar_tensor_tensor(out=x_tile(t0 + j), in0=a_bank[(2 + j) % 4][:, 0:D], scalar=rattn[:, j:j + 1],
                                                       in1=x_tile(t0 + j), op0=ALU.mult, op1=ALU.add)
                i.then_inc(s_projected, 1)

            def attention_norm_stats(a):
                after(alone=True)
                wait_alone(dve, s_added, (a + 1) * GT)
                norm_stats(a * GT, s_avar, astats, amv)

            def attention_norm(a):
                ta = a * GT
                norm(ta, a, xa, amv, astd, arstd, s_avar, s_astd, s_xa)
                dve.wait_ge(s_xa, (a + 1) * GT)
                done.add(nc.vector.tensor_tensor(x_res[:, bass.ds(ta, GT), :], x_res[:, bass.ds(ta, GT), :],
                                                 bo_sb[:, None, :].broadcast_to([P, GT, D]), ALU.add))

            def sequence(a, g, last=False):
                after(alone=True)
                if a is not None:
                    attention_low(a)
                if g is not None:
                    tg = (g - GROUPS) * GT
                    wait_alone(dve, s_projected, g - (GROUPS - 1))
                    norm_stats(tg, s_var, stats, mv)
                    norm(tg, g, xn, mv, std, rstd, s_var, s_std, s_xn, g * 16)
                ahead = a is not None and not last
                if ahead:
                    combine(a * GT + GT, a * 16 + 32)
                if a is not None:
                    add_v_bias(a)
                if g is not None:
                    router_max(g, True)
                    routed_low(xnT, g, True)
                    route(g)
                if a is not None:
                    scores_max(a)
                if ahead:
                    attention_norm_stats(a + 1)
                if g is not None:
                    if not last:
                        shared_h(g, 0, True)
                    slots(g, False, True)
                    weights(tg)
                    if not last:
                        shared_h(g, 1, True)
                if ahead:
                    attention_norm(a + 1)
                if g is not None and not last:
                    shared_h(g, 2, True)
                if a is not None:
                    after()
                    add_out(a * GT, a)
                if g is not None and not last:
                    shared_add(tg, g)

            def last_group(g):
                tg = (g - GROUPS) * GT
                after(alone=True)
                wait_alone(dve, s_projected, g - (GROUPS - 1))
                norm_stats(tg, s_var, stats, mv)
                norm(tg, g, xn, mv, std, rstd, s_var, s_std, s_xn, g * 16)
                shared_h(g - 1, 0, False)
                router_max(g, False)
                routed_low(xaT, g, False)
                route(g)
                slots(g, False, False)
                shared_h(g - 1, 1, False)
                shared_h(g - 1, 2, False)
                weights(tg)
                shared_add(tg - GT, g - 1)
                shared_h(g, 0, False)
                shared_h(g, 1, False)
                list_over(1)
                shared_h(g, 2, False)
                shared_add(tg, g)

            def combine_last(pair):
                for i in range(2):
                    combine((pair * 2 + i) * GT, pair * 16 + (16, 0)[i] * GROUPS + 16, ((0, 1), (2,)),
                            last_back[i], (s_back, s_back_odd)[i])

            def start_positions():
                nc.vector.memset(before[:, :], 0.0).then_inc(s_before, 1)

            def repeated(count, start, body, per):
                first_n, base = done.n, done.base
                with dve.Fori(start, start + count) as i:
                    done.base = (i - start) * per if start else i * per
                    body(i)
                    assert done.n - first_n == per, done.n - first_n
                done.base, done.n = base, first_n + per * count

            nc.vector.memset(eps[:, :], EPS).then_inc(s_const, 1)
            nc.vector.memset(blank[:, :], float(NOWHERE)).then_inc(s_zeros, 1)
            nc.vector.memset(zeros, 0.0).then_inc(s_zeros, 1)
            done.add(nc.vector.memset(idx[:, :, E * CT:], 0))
            done.add(nc.vector.memset(probs[:, :, E:E + 2], -1.0))
            done.add(nc.vector.memset(chosen[:, :, TOP_K:8], -1.0))
            dve.wait_ge(s_const, CONSTS)
            dve.wait_ge(s_load, 16 * LOADS)
            nc.vector.tensor_scalar(bq_scaled[:, :], bqk_sb[:, 0:KD], float(D) ** -0.5, None, ALU.mult).then_inc(s_bq, 1)
            dve.wait_ge(s_x0, 16)

            start_positions()
            norm_stats(0, s_var, stats, mv)
            for n, (w, raw_w) in enumerate(zip((shg_sb, shu_sb), raw_small)):
                dve.wait_ge(s_small_high, n + 1)
                low(w[:, 1, :, :], raw_w, w[:, 0, :, :]).then_inc(s_small, 1)
            norm(0, 0, xn, mv, std, rstd, s_var, s_std, s_xn)
            dve.wait_ge(s_x, 16)
            ffn_in(0, 0, first=True)
            repeated(GROUPS - 2, 1, lambda g: ffn_in(g * GT, g), FFN_IN_OPS)
            ffn_in((GROUPS - 1) * GT, GROUPS - 1, last=True)
            list_over(0)
            shared_add((GROUPS - 1) * GT, GROUPS - 1)
            weights((GROUPS - 1) * GT)
            experts(0)

            start_positions()
            dve.wait_ge(s_load_attn, 16 * LOADS_ATTN)
            dve.wait_ge(s_wqkv_high, 1)
            low(wqkv_split[:, 1, :, :], wqkv_sb[:, :, :], wqkv_split[:, 0, :, :]).then_inc(s_wqkv, 1)
            combine(0, 16)
            attention_norm_stats(0)
            attention_norm(0)
            sequence(0, None)
            first = done.n
            repeated(GROUPS - 2, 1, lambda a: sequence(a, a + (GROUPS - 1)), SEQUENCE_OPS)
            sequence(GROUPS - 1, 2 * GROUPS - 2, last=True)
            last_group(2 * GROUPS - 1)
            experts(1)
            repeated(GROUPS // 2, 0, combine_last, 2 * (GT - 1) * (TOP_K - 1))


FFN_IN_OPS = 35
SEQUENCE_OPS = 62
_OUT = (B, S, D)


def kernel(L0_attn_hidden_states, L0_attn_w_qkv, L0_attn_b_qkv, L0_attn_w_out, L0_attn_b_out,
           L0_ffn_gate_w, L0_ffn_w_gate, L0_ffn_w_up, L0_ffn_w_down, L0_ffn_sh_gate, L0_ffn_sh_up, L0_ffn_sh_down):
    import concourse.bacc as bacc
    from concourse.bass_utils import run_bass_kernel_spmd

    def chunks(w, p=P):
        w = np.asarray(w).T
        return w.reshape(w.shape[0] // p, p, w.shape[1]).transpose(1, 0, 2)

    w_gu = np.concatenate([np.asarray(L0_ffn_w_gate), np.asarray(L0_ffn_w_up)], axis=1)
    w_gu = w_gu.transpose(0, 2, 1).reshape(E, KD, P, 2 * F).transpose(0, 2, 1, 3).reshape(E * P, KD, 2 * F)
    w_d = np.asarray(L0_ffn_w_down).transpose(0, 2, 1).reshape(E, 2, FH, D).transpose(0, 2, 1, 3).reshape(E * FH, 2, D)
    b = np.asarray(L0_attn_b_qkv)
    arrays = {
        "x": np.asarray(L0_attn_hidden_states).reshape(N, D),
        "wqkv": chunks(L0_attn_w_qkv),
        "woT": chunks(L0_attn_w_out),
        "bqk": b[0:2 * D].reshape(4, P).T,
        "bv": np.broadcast_to(b[2 * D:], (P, D)),
        "bo": np.broadcast_to(np.asarray(L0_attn_b_out), (P, D)),
        "gateT": chunks(L0_ffn_gate_w),
        "w_gu": w_gu,
        "w_d": w_d,
        "sh_g": chunks(L0_ffn_sh_gate),
        "sh_u": chunks(L0_ffn_sh_up),
        "sh_d": np.asarray(L0_ffn_sh_down).T,
    }
    arrays = {name: np.ascontiguousarray(a) for name, a in arrays.items()}
    nc = bacc.Bacc("TRN2", target_bir_lowering=False, num_devices=1)
    aps = {n: nc.dram_tensor(n, a.shape, mybir.dt.from_np(a.dtype), kind="ExternalInput").ap() for n, a in arrays.items()}
    out = nc.dram_tensor("out", (N, D), F32, kind="ExternalOutput").ap()
    build(nc, **aps, out=out)
    got = run_bass_kernel_spmd(nc, [arrays], core_ids=[0])
    return got.results[0]["out"].reshape(_OUT)
```
